# Optimizing a Trainium2 kernel written in Bass

```python
import numpy as np
import jax
import jax.numpy as jnp

def _softmax(x, axis=-1):
    return jax.nn.softmax(x, axis=axis)

def _gelu(x):
    return jax.nn.gelu(x, approximate=True)

def _silu(x):
    return jax.nn.silu(x)

def _sigmoid(x):
    return jax.nn.sigmoid(x)

def _layernorm(x, axis=-1, eps=1e-05):
    m = jnp.mean(x, axis=axis, keepdims=True)
    v = jnp.var(x, axis=axis, keepdims=True)
    return (x - m) / jnp.sqrt(v + eps)

def _scatter_add(tgt, idx, src, axis=0):
    return tgt.at[idx].add(src)

def _segment_sum(src, seg, n):
    return jax.ops.segment_sum(src, seg, n)
kernel_name = 'mk_decoder_postln_d1_seqx_r2_634e94'

def setup_inputs(seed: int=0):
    np.random.seed(seed)
    _w = jnp.asarray

    def _rec_inputs():
        import jax
        import jax.numpy as jnp
        _rk = jax.random.key(seed)
        x = -0.0005146 + 1 * jax.random.normal(jax.random.fold_in(_rk, 1), (2, 2048, 512), jnp.float32)
        _lenS = 2048 - jax.random.randint(jax.random.fold_in(_rk, 7), (2,), 0, max(1, 2048 // 4) + 1, jnp.int32)
        _lenS2 = 77 - jax.random.randint(jax.random.fold_in(_rk, 8), (2,), 0, max(1, 77 // 4) + 1, jnp.int32)
        _ctx_1024P = jax.random.normal(jax.random.fold_in(_rk, 11), (2, 16, 512), jnp.float32)
        _ctx_1024c = jax.random.dirichlet(jax.random.fold_in(_rk, 511), 0.3 * jnp.ones((16,), jnp.float32), (2, 77))
        _ctx_1024t = jnp.einsum('bsk,bkd->bsd', _ctx_1024c, _ctx_1024P)
        _ctx_1024t = _ctx_1024t * jax.lax.rsqrt(jnp.mean(jnp.square(_ctx_1024t)) + 1e-12) * 0.953939
        ctx_1024 = -0.000392918 + 0.999932 * (_ctx_1024t + 0.3 * jax.random.normal(jax.random.fold_in(_rk, 611), (2, 77, 512), jnp.float32))
        return (x, ctx_1024)
    x, ctx_1024 = _rec_inputs()

    def _L0_attn_setup():
        import jax, jax.numpy as jnp
        import numpy as np
        B, N, C = (2, 1024, 512)
        H = 16
        D = C // H
        key = jax.random.key(seed)
        ks = jax.random.split(key, 5)
        s = 0.02
        return {'x': jax.random.normal(ks[0], (B, N, C), dtype=jnp.float32), 'qkv_w': jax.random.normal(ks[1], (C, 3 * C), dtype=jnp.float32) * s, 'qkv_b': jax.random.normal(ks[2], (3 * C,), dtype=jnp.float32) * s, 'proj_w': jax.random.normal(ks[3], (C, C), dtype=jnp.float32) * s, 'proj_b': jax.random.normal(ks[4], (C,), dtype=jnp.float32) * s}
    _L0_attn_all = _L0_attn_setup()
    _L0_attn_in = {k: v for k, v in _L0_attn_all.items() if k in ('qkv_w', 'qkv_b', 'proj_w', 'proj_b')}
    del _L0_attn_all

    def _L0_xattn_setup():
        import jax, jax.numpy as jnp
        import numpy as np
        DIM = 512
        HEADS = 8
        DIM_HEAD = 64
        INNER = HEADS * DIM_HEAD
        SCALE = DIM_HEAD ** (-0.5)

        def layer_norm(x, g, b, eps=1e-05):
            mu = jnp.mean(x, axis=-1, keepdims=True)
            var = jnp.mean(jnp.square(x - mu), axis=-1, keepdims=True)
            return (x - mu) * jax.lax.rsqrt(var + eps) * g + b
        key = jax.random.key(seed)
        ks = jax.random.split(key, 8)
        B, N, M = (4, 2048, 256)
        x = jax.random.normal(ks[0], (B, N, DIM), dtype=jnp.float32)
        latents = jax.random.normal(ks[1], (B, M, DIM), dtype=jnp.float32)
        s = 1.0 / np.sqrt(DIM)
        Wq = jax.random.normal(ks[2], (DIM, INNER), dtype=jnp.float32) * s
        Wk = jax.random.normal(ks[3], (DIM, INNER), dtype=jnp.float32) * s
        Wv = jax.random.normal(ks[4], (DIM, INNER), dtype=jnp.float32) * s
        Wo = jax.random.normal(ks[5], (INNER, DIM), dtype=jnp.float32) * (1.0 / np.sqrt(INNER))
        bo = jnp.zeros((DIM,), dtype=jnp.float32)
        gx = jnp.ones((DIM,), dtype=jnp.float32)
        bx = jnp.zeros((DIM,), dtype=jnp.float32)
        gl = jnp.ones((DIM,), dtype=jnp.float32)
        bl = jnp.zeros((DIM,), dtype=jnp.float32)
        return {'x': x, 'latents': latents, 'Wq': Wq, 'Wk': Wk, 'Wv': Wv, 'Wo': Wo, 'bo': bo, 'gx': gx, 'bx': bx, 'gl': gl, 'bl': bl}
    _L0_xattn_all = _L0_xattn_setup()
    _L0_xattn_in = {k: v for k, v in _L0_xattn_all.items() if k in ('Wq', 'Wk', 'Wv', 'Wo', 'bo', 'gx', 'bx', 'gl', 'bl')}
    del _L0_xattn_all

    def _L0_ffn_setup():
        import math
        import jax, jax.numpy as jnp
        import numpy as np
        NUM_EXPERTS = 8
        CAPACITY_FACTOR = 1.5
        key = jax.random.key(seed)
        ks = jax.random.split(key, 4)
        B, T, D, F, E = (4, 1024, 512, 2048, NUM_EXPERTS)
        scale = 0.02
        return {'x': jax.random.normal(ks[0], (B, T, D), dtype=jnp.float32), 'router_w': jax.random.normal(ks[1], (E, D), dtype=jnp.float32) * scale, 'w1': jax.random.normal(ks[2], (E, D, F), dtype=jnp.float32) * scale, 'b1': jnp.zeros((E, F), dtype=jnp.float32), 'w2': jax.random.normal(ks[3], (E, F, D), dtype=jnp.float32) * scale, 'b2': jnp.zeros((E, D), dtype=jnp.float32)}
    _L0_ffn_all = _L0_ffn_setup()
    _L0_ffn_in = {k: v for k, v in _L0_ffn_all.items() if k in ('router_w', 'w1', 'b1', 'w2', 'b2')}
    del _L0_ffn_all
    return {'x': x, 'ctx_1024': ctx_1024, 'L0_attn_qkv_w': _L0_attn_in['qkv_w'], 'L0_attn_qkv_b': _L0_attn_in['qkv_b'], 'L0_attn_proj_w': _L0_attn_in['proj_w'], 'L0_attn_proj_b': _L0_attn_in['proj_b'], 'L0_xattn_Wq': _L0_xattn_in['Wq'], 'L0_xattn_Wk': _L0_xattn_in['Wk'], 'L0_xattn_Wv': _L0_xattn_in['Wv'], 'L0_xattn_Wo': _L0_xattn_in['Wo'], 'L0_xattn_bo': _L0_xattn_in['bo'], 'L0_xattn_gx': _L0_xattn_in['gx'], 'L0_xattn_bx': _L0_xattn_in['bx'], 'L0_xattn_gl': _L0_xattn_in['gl'], 'L0_xattn_bl': _L0_xattn_in['bl'], 'L0_ffn_router_w': _L0_ffn_in['router_w'], 'L0_ffn_w1': _L0_ffn_in['w1'], 'L0_ffn_b1': _L0_ffn_in['b1'], 'L0_ffn_w2': _L0_ffn_in['w2'], 'L0_ffn_b2': _L0_ffn_in['b2']}

def reference(x, ctx_1024, L0_attn_qkv_w, L0_attn_qkv_b, L0_attn_proj_w, L0_attn_proj_b, L0_xattn_Wq, L0_xattn_Wk, L0_xattn_Wv, L0_xattn_Wo, L0_xattn_bo, L0_xattn_gx, L0_xattn_bx, L0_xattn_gl, L0_xattn_bl, L0_ffn_router_w, L0_ffn_w1, L0_ffn_b1, L0_ffn_w2, L0_ffn_b2):
    import jax
    import jax.numpy as jnp

    def _L0_attn_ref(x, qkv_w, qkv_b, proj_w, proj_b):
        import jax, jax.numpy as jnp
        import numpy as np
        B, N, C = (2, 1024, 512)
        H = 16
        D = C // H
        b, n, c = x.shape
        scale = (c // H) ** (-0.5)
        qkv = x @ qkv_w + qkv_b
        qkv = qkv.reshape(b, n, 3, H, D)
        q, k, v = jnp.moveaxis(qkv, 2, 0)
        attn = jnp.einsum('bnhd,bmhd->bhnm', q, k) * scale
        attn = jax.nn.softmax(attn, axis=-1)
        out = jnp.einsum('bhnm,bmhd->bnhd', attn, v).reshape(b, n, c)
        out = out @ proj_w + proj_b
        return out

    def _L0_xattn_ref(x, latents, Wq, Wk, Wv, Wo, bo, gx, bx, gl, bl):
        import jax, jax.numpy as jnp
        import numpy as np
        DIM = 512
        HEADS = 8
        DIM_HEAD = 64
        INNER = HEADS * DIM_HEAD
        SCALE = DIM_HEAD ** (-0.5)

        def layer_norm(x, g, b, eps=1e-05):
            mu = jnp.mean(x, axis=-1, keepdims=True)
            var = jnp.mean(jnp.square(x - mu), axis=-1, keepdims=True)
            return (x - mu) * jax.lax.rsqrt(var + eps) * g + b
        B, N, _ = x.shape
        M = latents.shape[1]
        xn = layer_norm(x, gx, bx)
        ln = layer_norm(latents, gl, bl)
        q = (ln @ Wq).reshape(B, M, HEADS, DIM_HEAD) * SCALE
        k = (xn @ Wk).reshape(B, N, HEADS, DIM_HEAD)
        v = (xn @ Wv).reshape(B, N, HEADS, DIM_HEAD)
        sim = jnp.einsum('bmhd,bnhd->bhmn', q, k)
        attn = jax.nn.softmax(sim, axis=-1)
        out = jnp.einsum('bhmn,bnhd->bmhd', attn, v).reshape(B, M, INNER)
        return out @ Wo + bo

    def _L0_ffn_ref(x, router_w, w1, b1, w2, b2):
        import math
        import jax, jax.numpy as jnp
        import numpy as np
        NUM_EXPERTS = 8
        CAPACITY_FACTOR = 1.5
        B, T, D = x.shape
        E = router_w.shape[0]
        N = B * T
        C = max(math.ceil(CAPACITY_FACTOR * N / E), 1)
        x_flat = x.reshape(N, D)
        logits = x_flat @ router_w.T
        probs = jax.nn.softmax(logits, axis=-1)
        chosen_e = jnp.argmax(probs, axis=-1)
        chosen_p = jnp.max(probs, axis=-1)
        onehot = jax.nn.one_hot(chosen_e, E, dtype=jnp.float32)
        pos = jnp.take_along_axis(jnp.cumsum(onehot, axis=0), chosen_e[:, None], axis=1)[:, 0] - 1.0
        pos = pos.astype(jnp.int32)
        kept = pos < C
        pos_c = jnp.clip(pos, 0, C - 1)
        buf = jnp.zeros((E, C, D), dtype=x.dtype).at[chosen_e, pos_c].add(x_flat * kept[:, None].astype(x.dtype))
        h = jax.nn.gelu(jnp.einsum('ecd,edf->ecf', buf, w1) + b1[:, None, :], approximate=False)
        eo = jnp.einsum('ecf,efd->ecd', h, w2) + b2[:, None, :]
        y = eo[chosen_e, pos_c] * (chosen_p * kept.astype(x.dtype))[:, None]
        return y.reshape(B, T, D)
    x = _layernorm(x + _L0_attn_ref(x, L0_attn_qkv_w, L0_attn_qkv_b, L0_attn_proj_w, L0_attn_proj_b), axis=-1)
    x = _layernorm(x + _L0_xattn_ref(ctx_1024, x, L0_xattn_Wq, L0_xattn_Wk, L0_xattn_Wv, L0_xattn_Wo, L0_xattn_bo, L0_xattn_gx, L0_xattn_bx, L0_xattn_gl, L0_xattn_bl), axis=-1)
    x = _layernorm(x + _L0_ffn_ref(x, L0_ffn_router_w, L0_ffn_w1, L0_ffn_b1, L0_ffn_w2, L0_ffn_b2), axis=-1)
    return x

_drawn_inputs = setup_inputs


def setup_inputs(seed=0):
    import zlib

    import numpy as np

    out = dict(_drawn_inputs(seed))
    spreads = {'L0_xattn_bo': (0.0, 0.1),
     'L0_xattn_gx': (1.0, 0.2),
     'L0_xattn_bx': (0.0, 0.1),
     'L0_xattn_gl': (1.0, 0.2),
     'L0_xattn_bl': (0.0, 0.408),
     'L0_ffn_b1': (0.0, 0.66),
     'L0_ffn_b2': (0.0, 0.349)}
    factors = {'L0_attn_qkv_w': 8.0,
     'L0_attn_qkv_b': 6.195,
     'L0_attn_proj_w': 5.413,
     'L0_attn_proj_b': 13.367}
    for name, (base, spread) in spreads.items():
        noise = np.random.default_rng([zlib.crc32(name.encode()), seed]).standard_normal(out[name].shape)
        drawn = base * np.exp(spread * noise) if base else spread * noise
        out[name] = jnp.asarray(drawn.astype(out[name].dtype))
    for name, factor in factors.items():
        out[name] = (out[name] * factor).astype(out[name].dtype)
    return out
```

```python
from contextlib import ExitStack

import concourse.bass as bass
from concourse import mybir

F32 = mybir.dt.float32
F32R = mybir.dt.float32r
I32 = mybir.dt.int32
U32 = mybir.dt.uint32
ALU = mybir.AluOpType
ACT = mybir.ActivationFunctionType
AX_X = mybir.AxisListType.X

P = 128
BANK = 512


class Shapes:

    def __init__(self, x, ctx, w1):
        self.B, self.N, self.C = x.shape
        self.KC = self.C // P
        self.H, self.D = 16, self.C // 16
        self.G = self.C // P
        self.HG = P // self.D
        self.T = self.N // P
        self.NQ = self.N // BANK
        self.M = ctx.shape[1]
        self.XH, self.XD = 8, 64
        self.E, _, self.F = w1.shape
        self.TOK = self.B * self.N
        self.CAP = max(-(-3 * self.TOK // (2 * self.E)), 1)


def wait_alone(engine, sem, value, waited):
    engine.wait_ge(sem, value)
    engine.sem_inc(waited, 1)


class Stage:

    def __init__(self, nc, ctx, name):
        self.nc, self.ctx, self.name = nc, ctx, name

    def sb(self, name, shape, dt=F32):
        return self.ctx.enter_context(self.nc.sbuf_tensor(f"{self.name}_{name}", shape, dt))

    def ps(self, name, shape=(P, BANK), dt=F32):
        return self.ctx.enter_context(self.nc.psum_tensor(f"{self.name}_{name}", list(shape), dt))

    def sem(self, name):
        return self.ctx.enter_context(self.nc.semaphore(f"{self.name}_{name}"))

    def block(self):
        return self.ctx.enter_context(self.nc.Block())


def make_ident(pool, ident, zeroed, ready):
    pool.memset(ident[:, :], 0.0).then_inc(zeroed, 1)
    pool.wait_ge(zeroed, 1)
    pool.affine_select(out=ident[:, :], in_=ident[:, :], compare_op=ALU.not_equal, fill=1.0,
                       base=0, pattern=[[-1, P]], channel_multiplier=1).then_inc(ready, 1)


def transpose_x(nc, z, x, xT_dram):
    B, N, C, KC, T = z.B, z.N, z.C, z.KC, z.T
    RING = 4
    with ExitStack() as ctx:
        s = Stage(nc, ctx, "tx")
        xin = s.sb("xin", [P, RING, C])
        xT = s.sb("xT", [P, 2, KC, RING * P])
        ident = s.sb("ident", [P, P])
        bank = [s.ps(f"bank{i}") for i in range(RING)]
        in_x = [s.sem(f"in_x{i}") for i in range(RING)]
        ident0, ident_ready = s.sem("ident0"), s.sem("ident_ready")
        mm, copied = s.sem("mm"), s.sem("copied")
        out_x = [s.sem(f"out_x{i}") for i in range(2)]
        block = s.block()
        PAIRS = B * T // RING // 2
        x_rows = x.rearrange("b n c -> (b n) c")
        out_v = xT_dram.rearrange("b (k p) n -> b p k n", p=P)

        @block.gpsimd
        def _(pool):
            pool.memset(ident[:, :], 0.0).then_inc(ident0, 1)
            pool.wait_ge(ident0, 1)
            pool.affine_select(out=ident[:, :], in_=ident[:, :], compare_op=ALU.not_equal, fill=1.0,
                               base=0, pattern=[[-1, P]], channel_multiplier=1).then_inc(ident_ready, 1)

        @block.sync
        def _(sp):
            with sp.Fori(0, PAIRS) as i:
                for h in range(2):
                    for t in range(RING):
                        sp.wait_ge(mm, (i * 2 + h) * RING if t == 0 else (i * 2 + h) * RING)
                        sp.dma_start(xin[:, t, :], x_rows[bass.ds(((i * 2 + h) * RING + t) * P, P), :]).then_inc(in_x[t], 16)

        @block.tensor
        def _(pe):
            pe.wait_ge(ident_ready, 1)
            with pe.Fori(0, PAIRS) as i:
                for h in range(2):
                    for t in range(RING):
                        pe.wait_ge(in_x[t], (i * 2 + h + 1) * 16)
                        pe.wait_ge(copied, (i * 2 + h) * RING)
                        for k in range(KC):
                            last = pe.transpose(bank[t][:, k * P:(k + 1) * P], xin[:, t, k * P:(k + 1) * P], ident[:, :])
                        last.then_inc(mm, 1)

        @block.vector
        def _(dve):
            with dve.Fori(0, PAIRS) as i:
                for h in range(2):
                    dve.wait_ge(out_x[h], i * 16)
                    for t in range(RING):
                        dve.wait_ge(mm, (i * 2 + h) * RING + t + 1)
                        dve.tensor_copy(xT[:, h, :, t * P:(t + 1) * P],
                                        bank[t][:, :].rearrange("p (k q) -> p k q", k=KC)).then_inc(copied, 1)

        @block.scalar
        def _(act):
            per_b = T // RING
            with act.Fori(0, PAIRS) as i:
                for h in range(2):
                    u = act.snap(i * 2 + h)
                    act.wait_ge(copied, (u + 1) * RING)
                    dst = out_v[bass.ds(u // per_b, 1), :, :, bass.ds(u % per_b * BANK, BANK)]
                    act.dma_start(dst.rearrange("o p k n -> (o p) k n"), xT[:, h, :, :]).then_inc(out_x[h], 16)
            for h in range(2):
                act.wait_ge(out_x[h], PAIRS * 16)


def self_attention(nc, z, xT_dram, qkv_w, qkv_b, attnT_dram):
    B, N, C, KC, G, HG, D, T, NQ = z.B, z.N, z.C, z.KC, z.G, z.HG, z.D, z.T, z.NQ
    SCALE = float(D) ** -0.5
    UNITS = B * G
    QK = 3 * D
    AUG = QK + 2
    KQ = N // BANK
    TQ = BANK // P
    NMAX = TQ * HG * KQ
    PER_STEP = 5
    OPS = [(what, n) for n in range(NQ) for what in "kqv"]
    SPLITS = [o for o in OPS if o[0] != "v"]
    PER_CHUNK = len(OPS) // (NQ - 1)
    OP_AT = {(c, 1 + 3 * i): c * PER_CHUNK + i for c in range(NQ - 1) for i in range(PER_CHUNK)}
    MOVES = 3 * HG
    STEPS = T * NQ
    SCORES = STEPS * HG

    with ExitStack() as ctx:
        s = Stage(nc, ctx, "sa")
        xT = s.sb("xT", [P, 2, KC, BANK])
        w = s.sb("w", [P, KC, 3, P])
        qkb = s.sb("qkb", [P, 2, G])
        vb = s.sb("vb", [P, C])
        ident = s.sb("ident", [P, P])
        ones = s.sb("ones", [P, D])
        hilo = s.sb("hilo", [P, 2, 2, BANK], F32R)
        q_stack = s.sb("q_stack", [P, 2, HG, N], F32R)
        k_stack = s.sb("k_stack", [P, 2, HG, N], F32R)
        v = s.sb("v", [P, 2, T, P])
        prob = s.sb("prob", [P, 2, HG, BANK])
        part_max = s.sb("part_max", [P, TQ, HG, KQ])
        top = s.sb("top", [P, TQ, HG])
        shift = s.sb("shift", [P, TQ, HG, 2], F32R)
        shiftT = s.sb("shiftT", [2 * HG, BANK], F32R)
        sums_sb = s.sb("sums", [P, 2, BANK])
        recip = s.sb("recip", [P, BANK])
        attn = s.sb("attn", [P, 2, BANK])

        sc = [s.ps(f"sc{i}") for i in range(3)]
        mxp = [s.ps(f"mx{i}") for i in range(2)]
        pv = s.ps("pv")
        den = s.ps("den")
        misc = s.ps("misc")

        in_x = [s.sem(f"in_x{i}") for i in range(2)]
        in_w, in_b = s.sem("in_w"), s.sem("in_b")
        const_ready, ident0 = s.sem("const_ready"), s.sem("ident0")
        proj_mm, v_ready = s.sem("proj_mm"), s.sem("v_ready")
        hi_ready, hilo_ready = s.sem("hi_ready"), s.sem("hilo_ready")
        stacked = [s.sem(f"stacked{i}") for i in range(len(SPLITS))]
        max_mm, max_read = s.sem("max_mm"), s.sem("max_read")
        top_ready, shift_hi, shift_ready = s.sem("top_ready"), s.sem("shift_hi"), s.sem("shift_ready")
        shift_mm, shiftT_ready, shift_in = s.sem("shift_mm"), s.sem("shiftT_ready"), s.sem("shift_in")
        sc_mm, prob_ready = s.sem("sc_mm"), s.sem("prob_ready")
        pv_mm, sums_ready, attn_ready = s.sem("pv_mm"), s.sem("sums_ready"), s.sem("attn_ready")
        recip_ready = s.sem("recip_ready")
        attn_out = [s.sem(f"attn_out{i}") for i in range(2)]
        block = s.block()

        w_v = qkv_w.rearrange("(k p) (a c) -> p k a c", p=P, a=3)
        xT_v = xT_dram.rearrange("b (k p) n -> b p k n", p=P)

        def counts(engine, u):
            known = {}

            def at(per):
                if per not in known:
                    known[per] = engine.snap(u * per)
                return known[per]
            return at

        def zero(per):
            return 0

        @block.gpsimd
        def _(pool):
            pool.memset(ident[:, :], 0.0).then_inc(ident0, 1)
            pool.wait_ge(ident0, 1)
            pool.affine_select(out=ident[:, :], in_=ident[:, :], compare_op=ALU.not_equal, fill=1.0,
                               base=0, pattern=[[-1, P]], channel_multiplier=1).then_inc(const_ready, 1)

            def load_weights(done, g):
                pool.wait_ge(proj_mm, done(len(OPS)))
                for k in range(KC):
                    pool.dma_start(w[:, k, :, :], w_v[:, k, :, bass.ds(g * P, P)]).then_inc(in_w, 16)

            def load_x(done, b, n):
                if n >= 2:
                    pool.wait_ge(proj_mm, done(len(OPS)) + 3 * (n - 1))
                pool.dma_start(xT[:, n % 2, :, :], xT_v[bass.ds(b, 1), :, :, n * BANK:(n + 1) * BANK]
                               .rearrange("o p k n -> (o p) k n")).then_inc(in_x[n % 2], 16)

            load_weights(zero, 0)
            for n in range(NQ):
                load_x(zero, 0, n)
            with pool.Fori(0, UNITS // 2) as pair:
                for p in range(2):
                    at = counts(pool, pool.snap(pair * 2 + p))
                    nxt = pool.snap((pair * 2 + p + 1) % UNITS)
                    b, g = pool.snap(nxt // G), pool.snap(nxt % G)
                    load_weights(lambda per: at(per) + per, g)
                    load_x(lambda per: at(per) + per, b, 0)
                    for c in range(NQ):
                        if c + 1 < NQ:
                            load_x(lambda per: at(per) + per, b, c + 1)
                        pool.wait_ge(attn_out[c % 2], at(NQ // 2 * 16) + c // 2 * 16)
                        pool.wait_ge(recip_ready, at(TQ * NQ) + TQ * (c + 1))
                        pool.tensor_tensor(attn[:, c % 2, :], sums_sb[:, 0, :], recip[:, :], ALU.mult).then_inc(attn_ready, 1)

        @block.sync
        def _(sp):
            sp.dma_start(qkb[:, :, :], qkv_b[0:2 * C].rearrange("(a g p) -> p a g", a=2, p=P),
                         allow_slow_non_contiguous=True).then_inc(in_b, 16)
            sp.dma_start(vb[:, :], qkv_b[2 * C:3 * C].rearrange("(o c) -> o c", o=1).broadcast_to([P, C])).then_inc(in_b, 16)

            def stack_chunk(done, i, buf):
                what, n = SPLITS[i]
                sp.wait_ge(hilo_ready, done(len(SPLITS)) + i + 1)
                stack = q_stack if what == "q" else k_stack
                for j in range(HG):
                    for r, part in enumerate((0, 0, 1) if what == "q" else (0, 1, 0)):
                        sp.dma_start(stack[D * r:D * (r + 1), buf, j, n * BANK:(n + 1) * BANK].bitcast(F32),
                                     hilo[D * j:D * (j + 1), i % 2, part, :].bitcast(F32)).then_inc(stacked[i], 16)

            def shift_rows(n, c, buf):
                sp.wait_ge(shiftT_ready, n)
                for j in range(HG):
                    sp.dma_start(q_stack[QK:AUG, buf, j, c * BANK:(c + 1) * BANK].bitcast(F32),
                                 shiftT[2 * j:2 * j + 2, :].bitcast(F32)).then_inc(shift_in, 16)

            for i in range(len(SPLITS)):
                stack_chunk(zero, i, 0)
            shift_rows(1, 0, 0)
            with sp.Fori(0, UNITS // 2) as pair:
                for p in range(2):
                    u = sp.snap(pair * 2 + p)
                    at = counts(sp, u)
                    b, g = sp.snap(u // G), sp.snap(u % G)

                    def store(c):
                        sp.wait_ge(attn_ready, at(NQ) + c + 1)
                        dst = attnT_dram[bass.ds(b, 1), bass.ds(g * P, P), c * BANK:(c + 1) * BANK]
                        sp.dma_start(dst.rearrange("o p n -> (o p) n"), attn[:, c % 2, :]).then_inc(attn_out[c % 2], 16)

                    for c in range(NQ):
                        for kt in range(T):
                            if c >= 1 and kt == TQ + 4:
                                store(c - 1)
                            op = OP_AT.get((c, kt))
                            if op is not None and OPS[op] in SPLITS:
                                stack_chunk(lambda per: at(per) + per, SPLITS.index(OPS[op]), 1 - p)
                        shift_rows(at(NQ) + c + 2, (c + 1) % NQ, p if c + 1 < NQ else 1 - p)
                    store(NQ - 1)
            sp.wait_ge(shift_in, (UNITS * NQ + 1) * 16 * HG)
            for i in range(len(SPLITS)):
                sp.wait_ge(stacked[i], (UNITS + 1) * 16 * MOVES)
            for i in range(2):
                sp.wait_ge(attn_out[i], 16 * UNITS * NQ // 2)

        @block.scalar
        def _(act):
            with act.Fori(0, UNITS // 2) as pair:
                for p in range(2):
                    u = act.snap(pair * 2 + p)
                    at = counts(act, u)
                    for c in range(NQ):
                        for kt in range(T):
                            step = c * T + kt
                            for j in range(HG):
                                n = step * HG + j
                                act.wait_ge(sc_mm, at(SCORES) + n + 1)
                                if j == 0:
                                    act.wait_ge(pv_mm, at(STEPS) + step - 1 if step else at(STEPS))
                                act.activation(prob[:, kt % 2, j, :], sc[n % 3][:, :], ACT.Exp, scale=SCALE).then_inc(prob_ready, 1)
                        act.wait_ge(pv_mm, at(STEPS) + (c + 1) * T)
                        act.wait_ge(attn_ready, at(NQ) + c)
                        act.activation(sums_sb[:, 0, :], pv[:, :], ACT.Copy).then_inc(sums_ready, 1)
                        act.activation(sums_sb[:, 1, :], den[:, :], ACT.Copy).then_inc(sums_ready, 1)

        @block.vector
        def _(dve):
            dve.memset(ones[:, :], 1.0).then_inc(const_ready, 1)
            dve.memset(k_stack[QK:AUG, :, :, :].bitcast(F32), 1.0).then_inc(const_ready, 1)
            dve.wait_ge(in_b, 32)

            def leave_psum(done, o, g, buf):
                what, n = OPS[o]
                dve.wait_ge(proj_mm, done(len(OPS)) + o + 1)
                if what == "v":
                    bias = vb[:, bass.ds(g * P, P)].rearrange("p (o c) -> p o c", o=1).broadcast_to([P, TQ, P])
                    dve.tensor_tensor(v[:, buf, n * TQ:(n + 1) * TQ, :], misc[:, :].rearrange("p (t c) -> p t c", t=TQ),
                                      bias, ALU.add).then_inc(v_ready, 1)
                    return
                i = SPLITS.index(OPS[o])
                bias = qkb[:, 0 if what == "q" else 1, bass.ds(g, 1)]
                dve.wait_ge(stacked[i - 2], done(16 * MOVES) + (16 * MOVES if i >= 2 else 0))
                dve.tensor_scalar(hilo[:, i % 2, 0, :], misc[:, :], bias, None, ALU.add).then_inc(hi_ready, 1)
                dve.wait_ge(hi_ready, done(len(SPLITS)) + i + 1)
                dve.scalar_tensor_tensor(out=hilo[:, i % 2, 1, :], in0=misc[:, :], scalar=bias,
                                         in1=hilo[:, i % 2, 0, :].bitcast(F32), op0=ALU.add, op1=ALU.subtract).then_inc(hilo_ready, 1)

            def reduce_max(n, m):
                dve.wait_ge(max_mm, n + 1)
                q, j, k = m // (HG * KQ), m // KQ % HG, m % KQ
                dve.reduce_max(part_max[:, q, j, k:k + 1], mxp[m % 2][:, :], AX_X).then_inc(max_read, 1)

            def make_shift(reads, n, ins):
                dve.wait_ge(max_read, reads)
                dve.reduce_max(top[:, :, :], part_max[:, :, :, :], AX_X).then_inc(top_ready, 1)
                dve.wait_ge(shift_mm, n)
                dve.wait_ge(top_ready, n + 1)
                dve.tensor_scalar(shift[:, :, :, 0], top[:, :, :], -1.0, None, ALU.mult).then_inc(shift_hi, 1)
                dve.wait_ge(shift_hi, n + 1)
                dve.scalar_tensor_tensor(out=shift[:, :, :, 1], in0=top[:, :, :], scalar=-1.0,
                                         in1=shift[:, :, :, 0].bitcast(F32), op0=ALU.mult, op1=ALU.subtract).then_inc(shift_ready, 1)
                dve.wait_ge(shift_mm, n + 1)
                dve.wait_ge(shift_in, ins)
                dve.tensor_copy(shiftT[:, :], misc[0:2 * HG, :]).then_inc(shiftT_ready, 1)

            for o in range(len(OPS)):
                leave_psum(zero, o, 0, 0)
            for m in range(NMAX):
                reduce_max(m, m)
            make_shift(NMAX, 0, 0)
            with dve.Fori(0, UNITS // 2) as pair:
                for p in range(2):
                    u = dve.snap(pair * 2 + p)
                    at = counts(dve, u)
                    g_next = dve.snap((u + 1) % G)

                    def invert(c, q):
                        if q == 0:
                            dve.wait_ge(sums_ready, at(2 * NQ) + 2 * (c + 1))
                            dve.wait_ge(attn_ready, at(NQ) + c)
                        dve.reciprocal(recip[:, q * P:(q + 1) * P], sums_sb[:, 1, q * P:(q + 1) * P]).then_inc(recip_ready, 1)

                    for c in range(NQ):
                        m = 0
                        for kt in range(T):
                            for _i in range(PER_STEP):
                                if m < NMAX:
                                    reduce_max(at(NQ * NMAX) + (c + 1) * NMAX + m, m)
                                    m += 1
                            if c >= 1 and 1 <= kt <= TQ:
                                invert(c - 1, kt - 1)
                            if (c, kt) in OP_AT:
                                leave_psum(lambda per: at(per) + per, OP_AT[(c, kt)], g_next, 1 - p)
                        make_shift(at(NQ * NMAX) + (c + 2) * NMAX, at(NQ) + c + 1, at(NQ * 16 * HG) + (c + 1) * 16 * HG)
                    for q in range(TQ):
                        invert(NQ - 1, q)

        @block.tensor
        def _(pe):
            pe.wait_ge(const_ready, 3)

            def project(done, o):
                what, n = OPS[o]
                if o == 0:
                    pe.wait_ge(in_w, done(16 * KC) + 16 * KC)
                if o % 3 == 0:
                    pe.wait_ge(in_x[n % 2], done(NQ // 2 * 16) + (n // 2 + 1) * 16)
                if o:
                    if OPS[o - 1] in SPLITS:
                        pe.wait_ge(hilo_ready, done(len(SPLITS)) + SPLITS.index(OPS[o - 1]) + 1)
                    else:
                        pe.wait_ge(v_ready, done(NQ) + OPS[o - 1][1] + 1)
                if what == "v":
                    for t in range(TQ):
                        for k in range(KC):
                            last = pe.matmul(misc[:, t * P:(t + 1) * P], xT[:, n % 2, k, t * P:(t + 1) * P], w[:, k, 2, :],
                                             start=(k == 0), stop=(k == KC - 1))
                else:
                    for k in range(KC):
                        last = pe.matmul(misc[:, :], w[:, k, 0 if what == "q" else 1, :], xT[:, n % 2, k, :],
                                         start=(k == 0), stop=(k == KC - 1))
                last.then_inc(proj_mm, 1)

            def max_pass(n, m, c, buf):
                if m >= 2 or n is not m:
                    pe.wait_ge(max_read, n - 1)
                q, j, k = m // (HG * KQ), m // KQ % HG, m % KQ
                at = c * BANK + q * P
                pe.matmul(mxp[m % 2][:, :], q_stack[0:QK, buf, j, at:at + P], k_stack[0:QK, buf, j, k * BANK:(k + 1) * BANK],
                          start=True, stop=True).then_inc(max_mm, 1)

            def transpose_shift(n):
                pe.wait_ge(shift_ready, n + 1)
                for q in range(TQ):
                    last = pe.transpose(misc[0:2 * HG, q * P:(q + 1) * P],
                                        shift[:, q, :, :].bitcast(F32).rearrange("p j a -> p (j a)"), ident[:, :])
                last.then_inc(shift_mm, 1)

            for o in range(len(OPS)):
                project(zero, o)
            for i in range(len(SPLITS)):
                if SPLITS[i] == ("q", 0) or SPLITS[i][0] == "k":
                    pe.wait_ge(stacked[i], 16 * MOVES)
            for m in range(NMAX):
                max_pass(m, m, 0, 0)
            transpose_shift(0)

            with pe.Fori(0, UNITS // 2) as pair:
                for p in range(2):
                    u = pe.snap(pair * 2 + p)
                    at = counts(pe, u)

                    def sums(c, kt, out):
                        if out is pv:
                            pe.wait_ge(prob_ready, at(SCORES) + (c * T + kt + 1) * HG)
                            if kt == 0:
                                if c == 0:
                                    pe.wait_ge(v_ready, at(NQ) + NQ)
                                pe.wait_ge(sums_ready, at(2 * NQ) + 2 * c)
                        for j in range(HG):
                            weights = v[:, p, kt, D * j:D * (j + 1)] if out is pv else ones[:, :]
                            last = pe.matmul(out[D * j:D * (j + 1), :], weights, prob[:, kt % 2, j, :],
                                             start=(kt == 0), stop=(kt == T - 1))
                        if out is den:
                            last.then_inc(pv_mm, 1)

                    def score(c, kt, j):
                        n = (c * T + kt) * HG + j
                        pe.wait_ge(prob_ready, at(SCORES) + n - 2 if n >= 3 else at(SCORES))
                        pe.matmul(sc[n % 3][:, :], k_stack[0:AUG, p, j, kt * P:(kt + 1) * P],
                                  q_stack[0:AUG, p, j, c * BANK:(c + 1) * BANK], start=True, stop=True).then_inc(sc_mm, 1)

                    for c in range(NQ):
                        pe.wait_ge(shift_in, at(NQ * 16 * HG) + (c + 1) * 16 * HG)
                        if c + 1 < NQ:
                            pe.wait_ge(stacked[SPLITS.index(("q", c + 1))], at(16 * MOVES) + 16 * MOVES)
                        else:
                            for i in range(len(SPLITS)):
                                if SPLITS[i] == ("q", 0) or SPLITS[i][0] == "k":
                                    pe.wait_ge(stacked[i], at(16 * MOVES) + 2 * 16 * MOVES)
                        buf = p if c + 1 < NQ else 1 - p
                        m = 0
                        for kt in range(T):
                            for i in range(PER_STEP):
                                if m < NMAX:
                                    max_pass(at(NQ * NMAX) + (c + 1) * NMAX + m, m, (c + 1) % NQ, buf)
                                    m += 1
                                if i < HG:
                                    score(c, kt, i)
                                if i % 2 and kt >= 1:
                                    sums(c, kt - 1, (pv, den)[i // 2])
                            if (c, kt) in OP_AT:
                                project(lambda per: at(per) + per, OP_AT[(c, kt)])
                            if kt == T - 2:
                                transpose_shift(at(NQ) + c + 1)
                        sums(c, T - 1, pv)
                        sums(c, T - 1, den)


def cross_attention(nc, z, a):
    B, N, C, KC, M, E = z.B, z.N, z.C, z.KC, z.M, z.E
    XH, XD = z.XH, z.XD
    TQ = BANK // P
    NCH = z.TOK // BANK
    PER_B = N // BANK
    SCALE = float(XD) ** -0.5
    PAIR_M = 2 * M
    HP = XH // 2
    PER_BANK = 2
    EPS = 1e-5

    with ExitStack() as ctx:
        s = Stage(nc, ctx, "ca")
        wp, wq, wo = (s.sb(n, [P, KC, C]) for n in ("wp", "wq", "wo"))
        rw = s.sb("rw", [P, KC, E])
        rw_rows = s.sb("rw_rows", [E, C])
        pb, ob = s.sb("pb", [P, C]), s.sb("ob", [P, C])
        gl, bl, gx, bx = (s.sb(n, [P, KC]) for n in ("gl", "bl", "gx", "bx"))
        ident = s.sb("ident", [P, P])
        minus_half = s.sb("minus_half", [P, TQ])
        cin = s.sb("cin", [M, B, C])
        cmv = s.sb("cmv", [M, B, 2])
        cstat = s.sb("cstat", [M, B, 6])
        crstd = s.sb("crstd", [M, B, 1])
        cnT = s.sb("cnT", [P, KC, B, M])
        k_all = s.sb("k_all", [P, B, HP, PAIR_M])
        v_all = s.sb("v_all", [M, B, C])
        wkv = s.sb("wkv", [P, KC, C])
        k_cur = s.sb("k_cur", [P, HP, PAIR_M])
        v_cur = s.sb("v_cur", [M, C])

        aT = s.sb("aT", [P, 2, KC, BANK])
        xb = s.sb("xb", [P, TQ, C])
        r1 = s.sb("r1", [P, TQ, C])
        x1 = s.sb("x1", [P, 2, TQ, C])
        x1n = s.sb("x1n", [P, TQ, C])
        x1b = s.sb("x1b", [P, TQ, C])
        x1nT = s.sb("x1nT", [P, KC, BANK])
        qT = s.sb("qT", [P, HP, BANK])
        e_in = s.sb("e_in", [P, TQ, XH, M])
        prob = e_in
        pT = s.sb("pT", [M, XH, BANK])
        oT = s.sb("oT", [P, HP, BANK])
        r2 = s.sb("r2", [P, TQ, C])
        x2 = s.sb("x2", [P, TQ, C])
        x2T = s.sb("x2T", [P, KC, BANK])
        stat = s.sb("stat", [P, 3, TQ, 6])
        mv = s.sb("mv", [P, 3, TQ, 2])
        var_eps = s.sb("var_eps", [P, 3, TQ])
        rstd = s.sb("rstd", [P, 3, TQ])
        top = s.sb("top", [P, TQ, XH])
        total = s.sb("total", [P, TQ, XH])
        inv = s.sb("inv", [P, TQ, XH])

        bank = [s.ps(f"bank{i}") for i in range(8)]

        in_c, in_w, waited = s.sem("in_c"), s.sem("in_w"), s.sem("waited")
        in_wk, in_wv = s.sem("in_wk"), s.sem("in_wv")
        id0, idr = s.sem("id0"), s.sem("idr")
        pool_c, dve_c, act_c, pe_c = s.sem("pool_c"), s.sem("dve_c"), s.sem("act_c"), s.sem("pe_c")
        in_a = [s.sem(f"in_a{i}") for i in range(2)]
        in_x, out_x2 = s.sem("in_x"), s.sem("out_x2")
        mm1, mm2t, mm2, mm3, mm4t, mm4v, mm4, mm5t, mm5 = (
            s.sem(f"mm{i}") for i in ("1", "2t", "2", "3", "4t", "4v", "4", "5t", "5"))
        xb_ready, r1_ready, x1_ready, x1b_ready, x1n_ready, x1nT_ready, qT_ready = (
            s.sem(i) for i in ("xb_ready", "r1_ready", "x1_ready", "x1b_ready", "x1n_ready", "x1nT_ready", "qT_ready"))
        stat_ready, mv_ready, ve_ready, rstd_ready = (s.sem(i) for i in ("stat_ready", "mv_ready", "ve_ready", "rstd_ready"))
        kv_cur, top_ready, e_ready, exp_ready, total_ready, inv_ready, prob_ready = (
            s.sem(i) for i in ("kv_cur", "top_ready", "e_ready", "exp_ready", "total_ready", "inv_ready", "prob_ready"))
        pT_ready, oT_ready, r2_ready, x2_ready, x2T_ready, lg_ready = (
            s.sem(i) for i in ("pT_ready", "oT_ready", "r2_ready", "x2_ready", "x2T_ready", "lg_ready"))
        block = s.block()

        x_rows = a.x.rearrange("b n c -> (b n) c")
        aT_v = a.attnT.rearrange("b (k p) n -> b p k n", p=P)
        x2_rows = a.x2

        def col(v):
            return v.rearrange("(k p) -> p k", p=P)

        def over(v):
            return v.rearrange("(o c) -> o c", o=1).broadcast_to([P, C])

        def w_tiles(w):
            return w.rearrange("(k p) c -> p k c", p=P)

        @block.sync
        def _(sp):
            sp.dma_start(cin[:, :, :], a.ctx.rearrange("b m c -> m b c")).then_inc(in_c, 16)
            for dst, src in ((gx, a.gx), (bx, a.bx), (gl, a.gl), (bl, a.bl)):
                sp.dma_start(dst[:, :], col(src), allow_slow_non_contiguous=True).then_inc(in_c, 16)
            sp.dma_start(rw_rows[:, :], a.rw).then_inc(in_c, 16)
            sp.dma_start(wkv[:, :, :], w_tiles(a.Wk)).then_inc(in_wk, 16)
            sp.dma_start(pb[:, :], over(a.proj_b)).then_inc(in_w, 16)
            sp.dma_start(ob[:, :], over(a.bo)).then_inc(in_w, 16)
            for dst, src in ((wp, a.proj_w), (wq, a.Wq), (wo, a.Wo)):
                sp.dma_start(dst[:, :, :], w_tiles(src)).then_inc(in_w, 16)
            sp.wait_ge(pe_c, 2)
            sp.dma_start(wkv[:, :, :], w_tiles(a.Wv)).then_inc(in_wv, 16)

            def load(n, ch, par):
                sp.wait_ge(mm1, n * TQ)
                sp.dma_start(aT[:, par, :, :], aT_v[bass.ds(ch // PER_B, 1), :, :, bass.ds(ch % PER_B * BANK, BANK)]
                             .rearrange("o p k n -> (o p) k n")).then_inc(in_a[par], 16)
                sp.wait_ge(r1_ready, n * TQ)
                sp.dma_start(xb[:, :, :], x_rows[bass.ds(ch * BANK, BANK), :].rearrange("(t p) c -> p t c", p=P)).then_inc(in_x, 16)

            load(0, 0, 0)
            with sp.Fori(0, NCH // 2) as i:
                for par in range(2):
                    n = sp.snap(i * 2 + par)
                    nxt = sp.snap((n + 1) % NCH)
                    load(n + 1, nxt, 1 - par)
                    sp.wait_ge(x2_ready, (n + 1) * TQ)
                    sp.dma_start(x2_rows[bass.ds(n * BANK, BANK), :].rearrange("(t p) c -> p t c", p=P), x2[:, :, :]).then_inc(out_x2, 16)
            sp.wait_ge(out_x2, NCH * 16)

        @block.gpsimd
        def _(pool):
            pool.memset(ident[:, :], 0.0).then_inc(id0, 1)
            pool.wait_ge(id0, 1)
            pool.affine_select(out=ident[:, :], in_=ident[:, :], compare_op=ALU.not_equal, fill=1.0,
                               base=0, pattern=[[-1, P]], channel_multiplier=1).then_inc(idr, 1)
            pool.wait_ge(idr, 1)
            pool.memset(minus_half[:, :], -0.5).then_inc(pool_c, 1)
            pool.wait_ge(pool_c, 1)
            pool.wait_ge(dve_c, 4)
            pool.tensor_tensor(crstd[:, :, 0], cmv[:, :, 1], minus_half[0:M, 0:B], ALU.pow).then_inc(pool_c, 1)

            def rstds(which, k):
                pool.wait_ge(ve_ready, k + 1)
                pool.tensor_tensor(rstd[:, which, :], var_eps[:, which, :], minus_half[:, :], ALU.pow).then_inc(rstd_ready, 1)

            def add_bias1(n):
                pool.wait_ge(in_x, (n + 1) * 16)
                pool.tensor_tensor(xb[:, :, :], xb[:, :, :], pb[:, :].rearrange("p (o c) -> p o c", o=1).broadcast_to([P, TQ, C]), ALU.add).then_inc(xb_ready, 1)

            pool.wait_ge(in_w, 5 * 16)
            add_bias1(0)
            rstds(0, 0)
            rstds(1, 1)
            pool.wait_ge(act_c, 2)
            with pool.Fori(0, NCH // 2) as i:
                for par in range(2):
                    n = pool.snap(i * 2 + par)
                    b = pool.snap(n // PER_B)
                    pool.wait_ge(mm3, n * TQ)
                    pool.tensor_copy(k_cur[:, :, :], k_all[:, bass.ds(b, 1), :, :].rearrange("p o h m -> p (o h) m")).then_inc(kv_cur, 1)
                    pool.wait_ge(mm4v, n)
                    pool.wait_ge(kv_cur, 2 * n + 1)
                    pool.tensor_copy(v_cur[:, :], v_all[:, bass.ds(b, 1), :].rearrange("p o c -> p (o c)")).then_inc(kv_cur, 1)
                    pool.wait_ge(kv_cur, 2 * n + 2)
                    pool.wait_ge(x1_ready, (n + 1) * TQ)
                    pool.wait_ge(r2_ready, n * TQ)
                    pool.tensor_tensor(x1b[:, :, :], x1[:, par, :, :], ob[:, :].rearrange("p (o c) -> p o c", o=1).broadcast_to([P, TQ, C]), ALU.add).then_inc(x1b_ready, 1)
                    add_bias1(n + 1)
                    rstds(0, 3 * n + 2)
                    rstds(1, 3 * n + 3)
                    rstds(2, 3 * n + 4)

        @block.vector
        def _(dve):
            dve.memset(k_all[:, :, :, :], 0.0).then_inc(dve_c, 1)
            dve.wait_ge(in_c, 6 * 16)
            for b in range(B):
                dve.bn_stats(cstat[:, b, :], cin[:, b, :]).then_inc(dve_c, 1)
            dve.wait_ge(dve_c, 1 + B)
            dve.bn_aggr(cmv[:, 0, :], cstat[:, 0, :])
            dve.bn_aggr(cmv[:, 1, :], cstat[:, 1, :]).then_inc(mv_ready, 1)
            dve.wait_ge(mv_ready, 1)
            dve.tensor_scalar(cmv[:, :, 1], cmv[:, :, 1], EPS, None, ALU.add).then_inc(dve_c, 1)
            dve.wait_ge(pool_c, 2)
            for b in range(B):
                dve.tensor_scalar(cin[:, b, :], cin[:, b, :], cmv[:, b, 0:1], crstd[:, b, :], ALU.subtract, ALU.mult).then_inc(dve_c, 1)
            dve.wait_ge(pe_c, 1)
            for k in range(KC):
                dve.tensor_scalar(cnT[:, k, :, :], bank[k][:, 0:B * M].rearrange("p (b m) -> p b m", b=B),
                                  gx[:, k:k + 1], bx[:, k:k + 1], ALU.mult, ALU.add).then_inc(dve_c, 1)
            for k in range(KC):
                last = dve.tensor_copy(rw[:, k, :], bank[4][:, k * E:(k + 1) * E])
            last.then_inc(dve_c, 1)

            def stats(which, t, src, seq):
                dve.bn_stats(stat[:, which, t, :], src).then_inc(stat_ready, 1)
                wait_alone(dve, stat_ready, seq + 1, waited)
                dve.bn_aggr(mv[:, which, t, :], stat[:, which, t, :]).then_inc(mv_ready, 1)

            def var_plus_eps(which, k):
                dve.wait_ge(mv_ready, 1 + (k + 1) * TQ)
                dve.tensor_scalar(var_eps[:, which, :], mv[:, which, :, 1], EPS, None, ALU.add).then_inc(ve_ready, 1)
                dve.wait_ge(rstd_ready, k + 1)

            def step1(n, par, k):
                dve.wait_ge(xb_ready, n + 1)
                for t in range(TQ):
                    dve.wait_ge(mm1, n * TQ + t + 1)
                    dve.tensor_tensor(r1[:, t, :], bank[t % 2][:, :], xb[:, t, :], ALU.add).then_inc(r1_ready, 1)
                    dve.wait_ge(r1_ready, n * TQ + t + 1)
                    stats(0, t, r1[:, t, :], k * TQ + t)
                var_plus_eps(0, k)
                for t in range(TQ):
                    dve.tensor_scalar(x1[:, par, t, :], r1[:, t, :], mv[:, 0, t, 0:1], rstd[:, 0, t:t + 1], ALU.subtract, ALU.mult).then_inc(x1_ready, 1)
                for t in range(TQ):
                    dve.wait_ge(x1_ready, n * TQ + t + 1)
                    stats(1, t, x1[:, par, t, :], (k + 1) * TQ + t)
                var_plus_eps(1, k + 1)
                for t in range(TQ):
                    if t == 0:
                        dve.wait_ge(mm2t, n * KC)
                    dve.tensor_scalar(x1n[:, t, :], x1[:, par, t, :], mv[:, 1, t, 0:1], rstd[:, 1, t:t + 1], ALU.subtract, ALU.mult).then_inc(x1n_ready, 1)

            def step2(n):
                for k in range(KC):
                    dve.wait_ge(mm2t, n * KC + k + 1)
                    if k == 0:
                        dve.wait_ge(mm2, n * HP)
                    dve.tensor_scalar(x1nT[:, k, :], bank[k][:, :], gl[:, k:k + 1], bl[:, k:k + 1], ALU.mult, ALU.add).then_inc(x1nT_ready, 1)

            step1(0, 0, 0)
            step2(0)
            with dve.Fori(0, NCH // 2) as i:
                for par in range(2):
                    n = dve.snap(i * 2 + par)
                    for t in range(TQ):
                        dve.wait_ge(mm3, n * TQ + t + 1)
                        for h in range(2):
                            src = bank[2 * (t % 2) + h][:, 0:PER_BANK * PAIR_M].rearrange("p (h m) -> p h m", m=M)
                            dve.reduce_max(top[:, t, 4 * h:4 * h + 4], src, AX_X).then_inc(top_ready, 1)
                        dve.wait_ge(top_ready, (n * TQ + t + 1) * 2)
                        for h in range(2):
                            src = bank[2 * (t % 2) + h][:, 0:PER_BANK * PAIR_M].rearrange("p (h m) -> p h m", m=M)
                            sub = top[:, t, 4 * h:4 * h + 4].rearrange("p (h o) -> p h o", o=1).broadcast_to([P, 4, M])
                            dve.tensor_tensor(e_in[:, t, 4 * h:4 * h + 4, :], src, sub, ALU.subtract).then_inc(e_ready, 1)
                    for t in range(TQ):
                        dve.wait_ge(exp_ready, n * TQ + t + 1)
                        dve.reduce_sum(total[:, t, :], e_in[:, t, :, :], AX_X).then_inc(total_ready, 1)
                    dve.wait_ge(total_ready, (n + 1) * TQ)
                    dve.reciprocal(inv[:, :, :], total[:, :, :]).then_inc(inv_ready, 1)
                    dve.wait_ge(inv_ready, n + 1)
                    for t in range(TQ):
                        by = inv[:, t, :].rearrange("p (h o) -> p h o", o=1).broadcast_to([P, XH, M])
                        dve.tensor_tensor(prob[:, t, :, :], e_in[:, t, :, :], by, ALU.mult).then_inc(prob_ready, 1)
                    step1(n + 1, 1 - par, 3 * n + 2)
                    dve.wait_ge(x1b_ready, n + 1)
                    for t in range(TQ):
                        dve.wait_ge(mm4, n * TQ + t + 1)
                        dve.tensor_tensor(r2[:, t, :], bank[4 + t % 2][:, :], x1b[:, t, :], ALU.add).then_inc(r2_ready, 1)
                        dve.wait_ge(r2_ready, n * TQ + t + 1)
                        stats(2, t, r2[:, t, :], (3 * n + 4) * TQ + t)
                    step2(n + 1)
                    var_plus_eps(2, 3 * n + 4)
                    dve.wait_ge(out_x2, n * 16)
                    dve.wait_ge(mm5t, n * KC)
                    for t in range(TQ):
                        dve.tensor_scalar(x2[:, t, :], r2[:, t, :], mv[:, 2, t, 0:1], rstd[:, 2, t:t + 1], ALU.subtract, ALU.mult).then_inc(x2_ready, 1)
                    dve.wait_ge(mm5, n + 1)
                    dve.tensor_copy(a.logits[:, bass.ds(n * TQ, TQ), :], bank[7][:, 0:TQ * E].rearrange("p (t e) -> p t e", e=E)).then_inc(lg_ready, 1)

        @block.scalar
        def _(act):
            act.wait_ge(pe_c, 2)
            act.wait_ge(dve_c, 1)
            for h in range(HP):
                for half in range(2):
                    rows = slice(half * XD, (half + 1) * XD)
                    last = act.activation(k_all[rows, :, h, half * M:(half + 1) * M],
                                          bank[h][rows, 0:B * M].rearrange("p (b m) -> p b m", b=B), ACT.Copy)
            last.then_inc(act_c, 1)
            act.wait_ge(pe_c, 3)
            for b in range(B):
                last = act.activation(v_all[:, b, :], bank[4 + b][0:M, :], ACT.Copy)
            last.then_inc(act_c, 1)

            def q_out(n):
                for h in range(HP):
                    act.wait_ge(mm2, n * HP + h + 1)
                    if h == 0:
                        act.wait_ge(mm3, n * TQ)
                    act.activation(qT[:, h, :], bank[4 + h % 2][:, :], ACT.Copy).then_inc(qT_ready, 1)

            q_out(0)
            with act.Fori(0, NCH // 2) as i:
                for par in range(2):
                    n = act.snap(i * 2 + par)
                    for t in range(TQ):
                        act.wait_ge(e_ready, (n * TQ + t + 1) * 2)
                        act.activation(e_in[:, t, :, :], e_in[:, t, :, :], ACT.Exp, scale=SCALE).then_inc(exp_ready, 1)
                    for t in range(TQ):
                        act.wait_ge(mm4t, n * TQ + t + 1)
                        if t == 0:
                            act.wait_ge(mm4v, n)
                        for h in range(2):
                            act.activation(pT[:, 4 * h:4 * h + 4, t * P:(t + 1) * P],
                                           bank[2 + 2 * (t % 2) + h][0:M, :].rearrange("m (h q) -> m h q", h=4), ACT.Copy).then_inc(pT_ready, 1)
                    act.wait_ge(mm4v, n + 1)
                    act.wait_ge(mm4, n * TQ)
                    for h in range(HP):
                        act.activation(oT[:, h, :], bank[(6, 7, 2, 3)[h]][:, :], ACT.Copy).then_inc(oT_ready, 1)
                    q_out(n + 1)
                    act.wait_ge(mm5, n)
                    for k in range(KC):
                        act.wait_ge(mm5t, n * KC + k + 1)
                        act.activation(x2T[:, k, :], bank[k][:, :], ACT.Copy).then_inc(x2T_ready, 1)

        @block.tensor
        def _(pe):
            pe.wait_ge(idr, 1)
            pe.wait_ge(dve_c, 2 + B + B)
            for k in range(KC):
                for b in range(B):
                    pe.transpose(bank[k][:, b * M:(b + 1) * M], cin[:, b, k * P:(k + 1) * P], ident[0:M, 0:M])
            for k in range(KC):
                last = pe.transpose(bank[4][:, k * E:(k + 1) * E], rw_rows[:, k * P:(k + 1) * P], ident[0:E, 0:E])
            last.then_inc(pe_c, 1)
            pe.wait_ge(dve_c, 2 + 2 * B + KC + 1)
            pe.wait_ge(in_wk, 16)
            for h in range(HP):
                for k in range(KC):
                    last = pe.matmul(bank[h][:, 0:B * M], wkv[:, k, h * P:(h + 1) * P], cnT[:, k, :, :].rearrange("p b m -> p (b m)"),
                                     start=(k == 0), stop=(k == KC - 1))
            last.then_inc(pe_c, 1)
            pe.wait_ge(in_wv, 16)
            for b in range(B):
                for k in range(KC):
                    last = pe.matmul(bank[4 + b][0:M, :], cnT[:, k, b, :], wkv[:, k, :], start=(k == 0), stop=(k == KC - 1))
            last.then_inc(pe_c, 1)
            pe.wait_ge(act_c, 2)
            pe.wait_ge(in_w, 5 * 16)

            def step1(n, par):
                pe.wait_ge(in_a[par], (n // 2 + 1) * 16)
                for t in range(TQ):
                    if t >= 2:
                        pe.wait_ge(r1_ready, n * TQ + t - 1)
                    for k in range(KC):
                        last = pe.matmul(bank[t % 2][:, :], aT[:, par, k, t * P:(t + 1) * P], wp[:, k, :], start=(k == 0), stop=(k == KC - 1))
                    last.then_inc(mm1, 1)

            def step2(n):
                pe.wait_ge(x1n_ready, (n + 1) * TQ)
                for k in range(KC):
                    for t in range(TQ):
                        last = pe.transpose(bank[k][:, t * P:(t + 1) * P], x1n[:, t, k * P:(k + 1) * P], ident[:, :])
                    last.then_inc(mm2t, 1)
                pe.wait_ge(x1nT_ready, (n + 1) * KC)
                for h in range(HP):
                    if h >= 2:
                        pe.wait_ge(qT_ready, n * HP + h - 1)
                    for k in range(KC):
                        last = pe.matmul(bank[4 + h % 2][:, :], wq[:, k, h * P:(h + 1) * P], x1nT[:, k, :], start=(k == 0), stop=(k == KC - 1))
                    last.then_inc(mm2, 1)

            step1(0, 0)
            step2(0)
            with pe.Fori(0, NCH // 2) as i:
                for par in range(2):
                    n = pe.snap(i * 2 + par)
                    pe.wait_ge(qT_ready, (n + 1) * HP)
                    pe.wait_ge(kv_cur, 2 * n + 2)
                    pe.wait_ge(x2T_ready, n * KC)
                    for t in range(TQ):
                        if t >= 2:
                            pe.wait_ge(e_ready, (n * TQ + t - 1) * 2)
                        for h in range(HP):
                            last = pe.matmul(bank[2 * (t % 2) + h // 2][:, h % 2 * PAIR_M:(h % 2 + 1) * PAIR_M],
                                             qT[:, h, t * P:(t + 1) * P], k_cur[:, h, :], start=True, stop=True)
                        last.then_inc(mm3, 1)
                    pe.wait_ge(e_ready, (n + 1) * 2 * TQ)
                    step1(n + 1, 1 - par)
                    for t in range(TQ):
                        pe.wait_ge(prob_ready, n * TQ + t + 1)
                        if t >= 2:
                            pe.wait_ge(pT_ready, (n * TQ + t - 1) * 2)
                        for h in range(XH):
                            last = pe.transpose(bank[2 + 2 * (t % 2) + h // 4][0:M, h % 4 * P:(h % 4 + 1) * P], prob[:, t, h, :], ident[:, :])
                        last.then_inc(mm4t, 1)
                    pe.wait_ge(pT_ready, (n + 1) * 2 * TQ)
                    pe.wait_ge(lg_ready, n)
                    for h in range(XH):
                        half = slice(h % 2 * XD, (h % 2 + 1) * XD)
                        last = pe.matmul(bank[(6, 7, 2, 3)[h // 2]][half, :], v_cur[:, h * XD:(h + 1) * XD], pT[:, h, :], start=True, stop=True)
                    last.then_inc(mm4v, 1)
                    pe.wait_ge(oT_ready, (n + 1) * HP)
                    for t in range(TQ):
                        if t >= 2:
                            pe.wait_ge(r2_ready, n * TQ + t - 1)
                        for k in range(KC):
                            last = pe.matmul(bank[4 + t % 2][:, :], oT[:, k, t * P:(t + 1) * P], wo[:, k, :], start=(k == 0), stop=(k == KC - 1))
                        last.then_inc(mm4, 1)
                    pe.wait_ge(x1n_ready, (n + 2) * TQ)
                    for k in range(KC):
                        for t in range(TQ):
                            last = pe.transpose(bank[k][:, t * P:(t + 1) * P], x1n[:, t, k * P:(k + 1) * P], ident[:, :])
                        last.then_inc(mm2t, 1)
                    pe.wait_ge(x1nT_ready, (n + 2) * KC)
                    for h in range(HP):
                        if h < 2:
                            pe.wait_ge(r2_ready, n * TQ + 3 + h)
                        else:
                            pe.wait_ge(qT_ready, (n + 1) * HP + h - 1)
                        for k in range(KC):
                            last = pe.matmul(bank[4 + h % 2][:, :], wq[:, k, h * P:(h + 1) * P], x1nT[:, k, :], start=(k == 0), stop=(k == KC - 1))
                        last.then_inc(mm2, 1)
                    pe.wait_ge(x2_ready, (n + 1) * TQ)
                    for k in range(KC):
                        for t in range(TQ):
                            last = pe.transpose(bank[k][:, t * P:(t + 1) * P], x2[:, t, k * P:(k + 1) * P], ident[:, :])
                        last.then_inc(mm5t, 1)
                    pe.wait_ge(x2T_ready, (n + 1) * KC)
                    for t in range(TQ):
                        for k in range(KC):
                            last = pe.matmul(bank[7][:, t * E:(t + 1) * E], x2T[:, k, t * P:(t + 1) * P], rw[:, k, :], start=(k == 0), stop=(k == KC - 1))
                    last.then_inc(mm5, 1)


def route(nc, z, a):
    E, CAP, NT = z.E, z.CAP, z.TOK // P
    SLOTS = E * CAP
    ST = SLOTS // P
    SKIP = 2 ** 20

    with ExitStack() as ctx:
        s = Stage(nc, ctx, "rt")
        iota_i = s.sb("iota_i", [P, NT, E], I32)
        iota_e = s.sb("iota_e", [P, NT, E])
        token = s.sb("token", [P, NT], I32)
        ident = s.sb("ident", [P, P])
        before = s.sb("before", [P, P])
        ones = s.sb("ones", [P, P])
        top, total, best, place = (s.sb(n, [P, NT]) for n in ("top", "total", "best", "place"))
        kept, weight, slot_f, skip_f = (s.sb(n, [P, NT]) for n in ("kept", "weight", "slot_f", "skip_f"))
        skip_i = s.sb("skip_i", [P, NT], I32)
        lx, ex, hot, cand, at_tile = (s.sb(n, [P, NT, E]) for n in ("lx", "ex", "hot", "cand", "at_tile"))
        zeros = s.sb("zeros", [P, NT])
        zero_i = s.sb("zero_i", [ST, P], I32)
        rows_i = s.sb("rows_i", [ST, P], I32)
        rows_f = s.sb("rows_f", [ST, P])
        in_tile, tiles, tabT = s.ps("in_tile"), s.ps("tiles"), s.ps("tabT")

        made, step, exp_ready, mm = s.sem("made"), s.sem("step"), s.sem("exp_ready"), s.sem("mm")
        table0, scattered, table_in = s.sem("table0"), s.sem("scattered"), s.sem("table_in")
        block = s.block()
        SLOTS_KNOWN = 20 + E
        table_rows = a.table.rearrange("(r c) o -> r (c o)", c=P)

        @block.gpsimd
        def _(pool):
            done = [0]

            def then(instruction):
                instruction.then_inc(made, 1)
                done[0] += 1
                pool.wait_ge(made, done[0])

            then(pool.memset(zero_i[:, :], 0))
            pool.dma_start(table_rows, zero_i[:, :]).then_inc(table0, 16)
            then(pool.iota(iota_i[:, :, :], pattern=[[0, NT], [1, E]], base=0, channel_multiplier=0))
            then(pool.iota(token[:, :], pattern=[[P, NT]], base=0, channel_multiplier=1))
            then(pool.memset(ones[:, :], 1.0))
            then(pool.affine_select(out=before[:, :], in_=ones[:, :], compare_op=ALU.is_gt, fill=0.0,
                                    base=0, pattern=[[1, P]], channel_multiplier=-1))
            then(pool.memset(ident[:, :], 0.0))
            then(pool.affine_select(out=ident[:, :], in_=ident[:, :], compare_op=ALU.not_equal, fill=1.0,
                                    base=0, pattern=[[-1, P]], channel_multiplier=1))
            pool.wait_ge(step, SLOTS_KNOWN)
            pool.wait_ge(table0, 16)
            for t in range(NT):
                pool.indirect_dma_start(a.table, bass.IndirectOffsetOnAxis(ap=skip_i[:, t:t + 1], axis=0),
                                        token[:, t:t + 1], None, bounds_check=SLOTS - 1, oob_is_err=False).then_inc(scattered, 16)
            pool.wait_ge(scattered, 16 * NT)
            pool.dma_start(rows_i[:, :], table_rows).then_inc(table_in, 16)
            pool.wait_ge(table_in, 16)

        @block.vector
        def _(dve):
            done = [0]

            def then(instruction):
                instruction.then_inc(step, 1)
                done[0] += 1
                dve.wait_ge(step, done[0])

            def each(v):
                return v[:, :].rearrange("p (t o) -> p t o", o=1).broadcast_to([P, NT, E])

            dve.wait_ge(made, 7)
            then(dve.tensor_copy(iota_e[:, :, :], iota_i[:, :, :]))
            then(dve.memset(zeros[:, :], 0.0))
            then(dve.reduce_max(top[:, :], a.logits[:, :, :], AX_X))
            then(dve.tensor_tensor(lx[:, :, :], a.logits[:, :, :], each(top), ALU.subtract))
            then(dve.tensor_scalar(cand[:, :, :], lx[:, :, :], 0.0, float(E), ALU.is_lt, ALU.mult))
            then(dve.tensor_tensor(cand[:, :, :], cand[:, :, :], iota_e[:, :, :], ALU.add))
            then(dve.tensor_reduce(best[:, :], cand[:, :, :], AX_X, ALU.min))
            then(dve.tensor_tensor(hot[:, :, :], iota_e[:, :, :], each(best), ALU.is_equal))
            assert done[0] == 8
            dve.wait_ge(exp_ready, 1)
            then(dve.reduce_sum(total[:, :], ex[:, :, :], AX_X))
            then(dve.reciprocal(weight[:, :], total[:, :]))
            dve.wait_ge(mm, 1)
            for e in range(E):
                then(dve.tensor_tensor_scan(at_tile[:, :, e], tiles[:, 0:NT * E].rearrange("p (t e) -> p t e", e=E)[:, :, e], zeros[:, :],
                                            0.0, ALU.add, ALU.add))
            then(dve.tensor_tensor(at_tile[:, :, :], at_tile[:, :, :], tiles[:, 0:NT * E].rearrange("p (t e) -> p t e", e=E), ALU.subtract))
            then(dve.tensor_tensor(at_tile[:, :, :], at_tile[:, :, :], in_tile[:, 0:NT * E].rearrange("p (t e) -> p t e", e=E), ALU.add))
            then(dve.tensor_tensor(at_tile[:, :, :], at_tile[:, :, :], hot[:, :, :], ALU.mult))
            then(dve.reduce_sum(place[:, :], at_tile[:, :, :], AX_X))
            then(dve.tensor_scalar(kept[:, :], place[:, :], float(CAP), None, ALU.is_lt))
            then(dve.tensor_scalar(slot_f[:, :], place[:, :], float(CAP - 1), None, ALU.min))
            then(dve.scalar_tensor_tensor(out=slot_f[:, :], in0=best[:, :], scalar=float(CAP), in1=slot_f[:, :], op0=ALU.mult, op1=ALU.add))
            then(dve.tensor_scalar(skip_f[:, :], kept[:, :], -float(SKIP), float(SKIP), ALU.mult, ALU.add))
            then(dve.tensor_tensor(skip_f[:, :], skip_f[:, :], slot_f[:, :], ALU.add))
            then(dve.tensor_copy(skip_i[:, :], skip_f[:, :]))
            assert done[0] == SLOTS_KNOWN
            then(dve.tensor_copy(a.slots[:, :], slot_f[:, :]))
            then(dve.tensor_tensor(a.weights[:, :], weight[:, :], kept[:, :], ALU.mult))
            dve.wait_ge(table_in, 16)
            then(dve.tensor_copy(rows_f[:, :], rows_i[:, :]))
            dve.wait_ge(mm, 2)
            then(dve.tensor_copy(a.tokens[:, :], tabT[:, 0:ST]))

        @block.scalar
        def _(act):
            act.wait_ge(step, 4)
            act.activation(ex[:, :, :], lx[:, :, :], ACT.Exp).then_inc(exp_ready, 1)

        @block.tensor
        def _(pe):
            pe.wait_ge(made, 7)
            pe.wait_ge(step, 8)
            cols = hot[:, :, :].rearrange("p t e -> p (t e)")
            pe.matmul(in_tile[:, 0:NT * E], before[:, :], cols, start=True, stop=True)
            pe.matmul(tiles[:, 0:NT * E], ones[:, :], cols, start=True, stop=True).then_inc(mm, 1)
            pe.wait_ge(step, SLOTS_KNOWN + 3)
            pe.transpose(tabT[:, 0:ST], rows_f[:, :], ident[0:ST, 0:ST]).then_inc(mm, 1)


def experts(nc, z, a):
    E, CAP, C, KC, F = z.E, z.CAP, z.C, z.KC, z.F
    TS = CAP // P
    HALF = CAP // 2
    STEPS = F // P
    QUADS = STEPS // 4
    PARTS = ((0, 0), (0, 1), (1, 0))
    FREE = 2

    with ExitStack() as ctx:
        s = Stage(nc, ctx, "ex")
        ident = s.sb("ident", [P, P])
        b1_rows = s.sb("b1_rows", [E * STEPS, P])
        b1 = s.sb("b1", [P, E * STEPS])
        b2 = s.sb("b2", [P, C])
        index = s.sb("index", [P, TS], I32)
        xg = s.sb("xg", [P, TS, C])
        xT = s.sb("xT", [P, 2, KC, CAP], F32R)
        w1_in = s.sb("w1_in", [P, 2, KC, 2 * P])
        w2_in = s.sb("w2_in", [P, 2, 2, C])
        w1 = s.sb("w1", [P, 2, 2, KC, P], F32R)
        w2 = s.sb("w2", [P, 2, 2, C], F32R)
        h = s.sb("h", [P, 2, CAP])
        hT = s.sb("hT", [P, 2, 2, CAP], F32R)
        out = s.sb("out", [P, TS, C])
        h_bank = [s.ps(f"h{i}") for i in range(2)]
        acc = [s.ps(f"acc{i}") for i in range(TS)]

        ident0, ident_ready = s.sem("ident0"), s.sem("ident_ready")
        in_b1, in_b2, b1_mm, b1_ready = s.sem("in_b1"), s.sem("in_b2"), s.sem("b1_mm"), s.sem("b1_ready")
        index_ready, gathered, waited = s.sem("index_ready"), s.sem("gathered"), s.sem("waited")
        x_mm, x_hi, x_ready = s.sem("x_mm"), s.sem("x_hi"), s.sem("x_ready")
        w_in = [s.sem(f"w_in{i}") for i in range(2)]
        w1_hi, w1_ready, w2_hi, w2_ready = s.sem("w1_hi"), s.sem("w1_ready"), s.sem("w2_hi"), s.sem("w2_ready")
        h_mm, h_ready, hT_hi, hT_ready = s.sem("h_mm"), s.sem("h_ready"), s.sem("hT_hi"), s.sem("hT_ready")
        o_mm, out_ready, stored = s.sem("o_mm"), s.sem("out_ready"), s.sem("stored")
        block = s.block()

        w1_v = a.w1.rearrange("e (k p) f -> e p k f", p=P)
        w2_v = a.w2.rearrange("e (i j p) c -> (e i) p j c", j=2, p=P)

        @block.sync
        def _(sp):
            sp.dma_start(b1_rows[:, :], a.b1.rearrange("e (i p) -> (e i) p", p=P)).then_inc(in_b1, 16)
            with sp.Fori(0, E) as e:
                sp.wait_ge(out_ready, e * TS)
                sp.dma_start(b2[:, :], a.b2[bass.ds(e, 1), :].broadcast_to([P, C])).then_inc(in_b2, 16)
                with sp.Fori(0, QUADS) as q:
                    eq = sp.snap(e * QUADS + q)
                    for buf in range(2):
                        sp.wait_ge(w1_ready, eq * 4)
                        sp.wait_ge(w2_ready, eq * 4)
                        sp.dma_start(w1_in[:, buf, :, :],
                                     w1_v[bass.ds(e, 1), :, :, bass.ds(q * (4 * P) + buf * 2 * P, 2 * P)]
                                     .rearrange("o p k f -> (o p) k f")).then_inc(w_in[buf], 16)
                        sp.dma_start(w2_in[:, buf, :, :], w2_v[bass.ds(eq * 2 + buf, 1), :, :, :]
                                     .rearrange("o p j c -> (o p) j c")).then_inc(w_in[buf], 16)

        @block.gpsimd
        def _(pool):
            make_ident(pool, ident, ident0, ident_ready)

            def gather(n, e):
                pool.wait_ge(x_mm, n * TS)
                pool.tensor_copy(index[:, :], a.tokens[:, bass.ds(e * TS, TS)]).then_inc(index_ready, 1)
                wait_alone(pool, index_ready, n + 1, waited)
                for t in range(TS):
                    pool.indirect_dma_start(xg[:, t, :], None, a.x2,
                                            bass.IndirectOffsetOnAxis(ap=index[:, t:t + 1], axis=0)).then_inc(gathered, 16)
                pool.wait_ge(gathered, (n + 1) * (TS * 16))

            gather(0, 0)
            with pool.Fori(0, E) as e:
                gather(pool.snap(e + 1), pool.snap((e + 1) % E))
                pool.wait_ge(out_ready, (e + 1) * TS)
                pool.dma_start(a.eo[bass.ds(e * CAP, CAP), :].rearrange("(t p) c -> p t c", p=P),
                               out[:, :, :]).then_inc(stored, 16)
            pool.wait_ge(stored, E * 16)

        @block.scalar
        def _(act):
            def high_x(n):
                for t in range(TS):
                    act.wait_ge(x_mm, n * TS + t + 1)
                    act.activation(xT[:, 0, :, t * P:(t + 1) * P], h_bank[t % 2][:, :].rearrange("p (k q) -> p k q", k=KC),
                                   ACT.Copy).then_inc(x_hi, 1)

            act.wait_ge(b1_ready, 1)
            high_x(0)
            with act.Fori(0, E) as e:
                with act.Fori(0, QUADS) as q:
                    eq = act.snap(e * QUADS + q)
                    n = act.snap(eq * 4)
                    n2 = act.snap(eq * 8)
                    for j in range(4):
                        if j % 2 == 0:
                            act.wait_ge(w_in[j // 2], (eq + 1) * 32)
                        cols = slice(j % 2 * P, (j % 2 + 1) * P)
                        act.wait_ge(h_mm, n2 + 2 * j - 2 + 2 * FREE)
                        act.activation(w1[:, j % 2, 0, :, :], w1_in[:, j // 2, :, cols], ACT.Copy).then_inc(w1_hi, 1)
                        act.wait_ge(o_mm, n + j - 1 + FREE)
                        act.activation(w2[:, j % 2, 0, :], w2_in[:, j // 2, j % 2, :], ACT.Copy).then_inc(w2_hi, 1)
                        for half in range(2):
                            act.wait_ge(h_mm, n2 + 2 * j + half + 2 * FREE + 1)
                            act.wait_ge(hT_ready, n2 + 2 * j + half - 3 + 2 * FREE)
                            act.activation(h[:, j % 2, half * HALF:(half + 1) * HALF], h_bank[half][:, 0:HALF], ACT.Gelu,
                                           bias=b1[:, bass.ds(n + j, 1)]).then_inc(h_ready, 1)
                high_x(act.snap(e + 1))

        @block.vector
        def _(dve):
            dve.sem_inc(hT_ready, 2 * FREE)
            dve.wait_ge(b1_mm, 1)
            dve.tensor_copy(b1[:, :], acc[0][:, 0:E * STEPS]).then_inc(b1_ready, 1)

            def low_x(n):
                for t in range(TS):
                    dve.wait_ge(x_hi, n * TS + t + 1)
                    cols = slice(t * P, (t + 1) * P)
                    dve.tensor_tensor(xT[:, 1, :, cols], h_bank[t % 2][:, :].rearrange("p (k q) -> p k q", k=KC),
                                      xT[:, 0, :, cols].bitcast(F32), ALU.subtract).then_inc(x_ready, 1)

            low_x(0)
            with dve.Fori(0, E) as e:
                with dve.Fori(0, QUADS) as q:
                    eq = dve.snap(e * QUADS + q)
                    n = dve.snap(eq * 4)
                    n2 = dve.snap(eq * 8)
                    for j in range(4):
                        cols = slice(j % 2 * P, (j % 2 + 1) * P)
                        dve.wait_ge(w1_hi, n + j + 1)
                        dve.tensor_tensor(w1[:, j % 2, 1, :, :], w1_in[:, j // 2, :, cols], w1[:, j % 2, 0, :, :].bitcast(F32), ALU.subtract).then_inc(w1_ready, 1)
                        dve.wait_ge(w2_hi, n + j + 1)
                        dve.tensor_tensor(w2[:, j % 2, 1, :], w2_in[:, j // 2, j % 2, :], w2[:, j % 2, 0, :].bitcast(F32), ALU.subtract).then_inc(w2_ready, 1)
                        dve.wait_ge(o_mm, n + j - 1 + FREE)
                        for half in range(2):
                            cols = slice(half * HALF, (half + 1) * HALF)
                            dve.wait_ge(h_ready, n2 + 2 * j + half + 1)
                            dve.tensor_copy(hT[:, j % 2, 0, cols], h[:, j % 2, cols]).then_inc(hT_hi, 1)
                            dve.wait_ge(hT_hi, n2 + 2 * j + half + 1)
                            dve.tensor_tensor(hT[:, j % 2, 1, cols], h[:, j % 2, cols], hT[:, j % 2, 0, cols].bitcast(F32), ALU.subtract).then_inc(hT_ready, 1)
                low_x(dve.snap(e + 1))
                dve.wait_ge(in_b2, (e + 1) * 16)
                dve.wait_ge(stored, e * 16)
                dve.wait_ge(o_mm, (e + 1) * STEPS + FREE)
                for t in range(TS):
                    dve.tensor_tensor(out[:, t, :], acc[t][:, :], b2[:, :], ALU.add).then_inc(out_ready, 1)

        @block.tensor
        def _(pe):
            pe.sem_inc(h_mm, 2 * FREE)
            pe.sem_inc(o_mm, FREE)
            pe.wait_ge(ident_ready, 1)
            pe.wait_ge(in_b1, 16)
            pe.transpose(acc[0][:, 0:E * STEPS], b1_rows[:, :], ident[0:E * STEPS, 0:E * STEPS]).then_inc(b1_mm, 1)

            def transpose_rows(n, t, first=False):
                if t == 0:
                    pe.wait_ge(gathered, (n + 1) * (TS * 16))
                if t >= 2:
                    pe.wait_ge(x_ready, n * TS + t - 1)
                elif not first:
                    pe.wait_ge(h_ready, n * (2 * STEPS))
                for k in range(KC):
                    last = pe.transpose(h_bank[t % 2][:, k * P:(k + 1) * P], xg[:, t, k * P:(k + 1) * P], ident[:, :])
                last.then_inc(x_mm, 1)

            def first_layer(n, n2, j, opens=False):
                pe.wait_ge(w1_ready, n + j + 1)
                for half in range(2):
                    if not opens:
                        pe.wait_ge(h_ready, n2 + 2 * j + half - 1)
                    for i, (pw, px) in enumerate(PARTS):
                        for k in range(KC):
                            last = pe.matmul(h_bank[half][:, 0:HALF], w1[:, j % 2, pw, k, :],
                                             xT[:, px, k, half * HALF:(half + 1) * HALF],
                                             start=(i == 0 and k == 0), stop=(i == 2 and k == KC - 1))
                    last.then_inc(h_mm, 1)

            def second_layer(n, n2, j, start=False, stop=False):
                pe.wait_ge(w2_ready, n + j + 1)
                pe.wait_ge(hT_ready, n2 + 2 * j + 2 + 2 * FREE)
                for t in range(TS):
                    for i, (ph, pw) in enumerate(PARTS):
                        last = pe.matmul(acc[t][:, :], hT[:, j % 2, ph, t * P:(t + 1) * P], w2[:, j % 2, pw, :],
                                         start=(start and i == 0), stop=(stop and i == 2))
                last.then_inc(o_mm, 1)

            for t in range(TS):
                transpose_rows(0, t, first=True)
            with pe.Fori(0, E) as e:
                pe.wait_ge(x_ready, (e + 1) * TS)
                n, n2 = pe.snap(e * STEPS), pe.snap(e * (2 * STEPS))
                first_layer(n, n2, 0, opens=True)
                for j in range(1, 4):
                    first_layer(n, n2, j)
                    if j == 1:
                        pe.wait_ge(out_ready, e * TS)
                    second_layer(n, n2, j - 1, start=(j == 1))
                with pe.Fori(1, QUADS) as q:
                    m, m2 = pe.snap((e * QUADS + q) * 4), pe.snap((e * QUADS + q) * 8)
                    for j in range(4):
                        first_layer(m, m2, j)
                        second_layer(m, m2, j - 1)
                nxt = pe.snap(e + 1)
                transpose_rows(nxt, 0)
                transpose_rows(nxt, 1)
                second_layer(n, n2, STEPS - 1, stop=True)
                for t in range(2, TS):
                    transpose_rows(nxt, t)


def combine(nc, z, a):
    C, NT = z.C, z.TOK // P
    TG = 4
    GROUPS = NT // TG
    EPS = 1e-5

    with ExitStack() as ctx:
        s = Stage(nc, ctx, "cb")
        index = s.sb("index", [P, 2, TG], I32)
        x2 = s.sb("x2", [P, 2, TG, C])
        y = s.sb("y", [P, 2, TG, C])
        r = s.sb("r", [P, 2, TG, C])
        o = s.sb("o", [P, 2, TG, C])
        stat = s.sb("stat", [P, 2, TG, 6])
        mv = s.sb("mv", [P, 2, TG, 2])
        var_eps, rstd = s.sb("var_eps", [P, 2, TG]), s.sb("rstd", [P, 2, TG])
        minus_half = s.sb("minus_half", [P, TG])

        in_x2 = [s.sem(f"in_x2{i}") for i in range(2)]
        in_y = [s.sem(f"in_y{i}") for i in range(2)]
        out_o = [s.sem(f"out_o{i}") for i in range(2)]
        half_ready, index_ready, r_ready, stat_ready = s.sem("half_ready"), s.sem("index_ready"), s.sem("r_ready"), s.sem("stat_ready")
        mv_ready, var_ready, rstd_ready, o_ready = s.sem("mv_ready"), s.sem("var_ready"), s.sem("rstd_ready"), s.sem("o_ready")
        waited = [s.sem("waited_dve"), s.sem("waited_pool")]
        block = s.block()
        rows = TG * P
        x2_v = a.x2.rearrange("(g t p) c -> g p t c", t=TG, p=P)
        out_v = a.out.rearrange("b n c -> (b n) c").rearrange("(g t p) c -> g p t c", t=TG, p=P)

        @block.sync
        def _(sp):
            with sp.Fori(0, GROUPS // 2) as i:
                for par in range(2):
                    sp.wait_ge(r_ready, i * (2 * TG))
                    sp.dma_start(x2[:, par, :, :], x2_v[bass.ds(i * 2 + par, 1), :, :, :]
                                 .rearrange("o p t c -> (o p) t c")).then_inc(in_x2[par], 16)

        @block.gpsimd
        def _(pool):
            pool.memset(minus_half[:, :], -0.5).then_inc(half_ready, 1)
            pool.wait_ge(half_ready, 1)
            with pool.Fori(0, GROUPS // 2) as i:
                pool.wait_ge(r_ready, i * (2 * TG))
                for par in range(2):
                    n = pool.snap(i * 2 + par)
                    pool.tensor_copy(index[:, par, :], a.slots[:, bass.ds(n * TG, TG)]).then_inc(index_ready, 1)
                    wait_alone(pool, index_ready, n + 1, waited[1])
                    for t in range(TG):
                        pool.indirect_dma_start(y[:, par, t, :], None, a.eo,
                                                bass.IndirectOffsetOnAxis(ap=index[:, par, t:t + 1], axis=0)).then_inc(in_y[par], 16)
                for par in range(2):
                    pool.wait_ge(var_ready, i * 2 + par + 1)
                    pool.tensor_tensor(rstd[:, par, :], var_eps[:, par, :], minus_half[:, :], ALU.pow).then_inc(rstd_ready, 1)

        @block.vector
        def _(dve):
            with dve.Fori(0, GROUPS // 2) as i:
                for par in range(2):
                    n = dve.snap(i * 2 + par)
                    dve.wait_ge(in_x2[par], (i + 1) * 16)
                    dve.wait_ge(in_y[par], (i + 1) * (16 * TG))
                    if par == 0:
                        dve.wait_ge(o_ready, i * (2 * TG))
                    for t in range(TG):
                        dve.scalar_tensor_tensor(out=r[:, par, t, :], in0=y[:, par, t, :],
                                                 scalar=a.weights[:, bass.ds(n * TG + t, 1)], in1=x2[:, par, t, :],
                                                 op0=ALU.mult, op1=ALU.add).then_inc(r_ready, 1)
                        dve.wait_ge(r_ready, n * TG + t + 1)
                        dve.bn_stats(stat[:, par, t, :], r[:, par, t, :]).then_inc(stat_ready, 1)
                        wait_alone(dve, stat_ready, n * TG + t + 1, waited[0])
                        dve.bn_aggr(mv[:, par, t, :], stat[:, par, t, :]).then_inc(mv_ready, 1)
                    dve.wait_ge(mv_ready, (n + 1) * TG)
                    dve.tensor_scalar(var_eps[:, par, :], mv[:, par, :, 1], EPS, None, ALU.add).then_inc(var_ready, 1)
                for par in range(2):
                    n = dve.snap(i * 2 + par)
                    dve.wait_ge(rstd_ready, n + 1)
                    dve.wait_ge(out_o[par], i * 16)
                    for t in range(TG):
                        dve.tensor_scalar(o[:, par, t, :], r[:, par, t, :], mv[:, par, t, 0:1], rstd[:, par, t:t + 1],
                                          ALU.subtract, ALU.mult).then_inc(o_ready, 1)

        @block.scalar
        def _(act):
            with act.Fori(0, GROUPS // 2) as i:
                for par in range(2):
                    act.wait_ge(o_ready, (i * 2 + par + 1) * TG)
                    act.dma_start(out_v[bass.ds(i * 2 + par, 1), :, :, :].rearrange("o p t c -> (o p) t c"),
                                  o[:, par, :, :]).then_inc(out_o[par], 16)
            for par in range(2):
                act.wait_ge(out_o[par], GROUPS // 2 * 16)


class Tensors:
    pass


def decoder_layer(nc, x, ctx_rows, qkv_w, qkv_b, proj_w, proj_b, Wq, Wk, Wv, Wo, bo, gx, bx, gl, bl,
                  router_w, w1, b1, w2, b2, out):
    z = Shapes(x, ctx_rows, w1)
    slots = z.E * z.CAP

    def scratch(name, shape, dt=F32):
        return nc.dram_tensor(name, shape, dt, kind="Internal").ap()

    xT = scratch("xT", (z.B, z.C, z.N))
    attnT = scratch("attnT", (z.B, z.C, z.N))
    transpose_x(nc, z, x, xT)
    self_attention(nc, z, xT, qkv_w, qkv_b, attnT)
    with ExitStack() as ctx:
        keep = Stage(nc, ctx, "keep")
        NT = z.TOK // P
        a = Tensors()
        a.x, a.ctx, a.attnT, a.out = x, ctx_rows, attnT, out
        a.proj_w, a.proj_b, a.Wq, a.Wk, a.Wv, a.Wo, a.bo = proj_w, proj_b, Wq, Wk, Wv, Wo, bo
        a.gx, a.bx, a.gl, a.bl, a.rw = gx, bx, gl, bl, router_w
        a.w1, a.b1, a.w2, a.b2 = w1, b1, w2, b2
        a.x2 = scratch("x2", (z.TOK, z.C))
        a.table = scratch("table", (slots, 1), I32)
        a.eo = scratch("eo", (slots, z.C))
        a.logits = keep.sb("logits", [P, NT, z.E])
        a.weights = keep.sb("weights", [P, NT])
        a.slots = keep.sb("slots", [P, NT], I32)
        a.tokens = keep.sb("tokens", [P, slots // P], I32)
        cross_attention(nc, z, a)
        route(nc, z, a)
        experts(nc, z, a)
        combine(nc, z, a)


_INS = ["x", "ctx_1024", "L0_attn_qkv_w", "L0_attn_qkv_b", "L0_attn_proj_w", "L0_attn_proj_b",
        "L0_xattn_Wq", "L0_xattn_Wk", "L0_xattn_Wv", "L0_xattn_Wo", "L0_xattn_bo", "L0_xattn_gx",
        "L0_xattn_bx", "L0_xattn_gl", "L0_xattn_bl", "L0_ffn_router_w", "L0_ffn_w1", "L0_ffn_b1",
        "L0_ffn_w2", "L0_ffn_b2"]
_OUTS = [((2, 2048, 512), "float32")]


def kernel(**inputs):
    import numpy as _np
    import concourse.bacc as _bacc
    from concourse import mybir as _mybir
    from concourse.bass_utils import run_bass_kernel_spmd as _run

    nc = _bacc.Bacc("TRN2", target_bir_lowering=False, num_devices=1)
    nc.disable_value_cache = True
    arrays, args = {}, []
    for name in _INS:
        a = _np.ascontiguousarray(inputs[name])
        arrays[f"in_{name}_dram"] = a
        args.append(nc.dram_tensor(f"in_{name}_dram", a.shape, _mybir.dt.from_np(a.dtype), kind="ExternalInput").ap())
    for i, (shape, dtype) in enumerate(_OUTS):
        dt = _mybir.dt.from_np(_np.dtype(dtype))
        args.append(nc.dram_tensor(f"out_{i}_dram", shape, dt, kind="ExternalOutput").ap())
    decoder_layer(nc, *args)
    r = _run(nc, [arrays], core_ids=[0])
    return r.results[0]["out_0_dram"]
```

```python
from contextlib import ExitStack

import concourse.bass as bass
from concourse import mybir

F32 = mybir.dt.float32
F32R = mybir.dt.float32r
I32 = mybir.dt.int32
U32 = mybir.dt.uint32
ALU = mybir.AluOpType
ACT = mybir.ActivationFunctionType
AX_X = mybir.AxisListType.X

P = 128
BANK = 512


class Shapes:

    def __init__(self, x, ctx, w1):
        self.B, self.N, self.C = x.shape
        self.KC = self.C // P
        self.H, self.D = 16, self.C // 16
        self.G = self.C // P
        self.HG = P // self.D
        self.T = self.N // P
        self.NQ = self.N // BANK
        self.M = ctx.shape[1]
        self.XH, self.XD = 8, 64
        self.E, _, self.F = w1.shape
        self.TOK = self.B * self.N
        self.CAP = max(-(-3 * self.TOK // (2 * self.E)), 1)


def wait_alone(engine, sem, value, waited):
    engine.wait_ge(sem, value)
    engine.sem_inc(waited, 1)


class Stage:

    def __init__(self, nc, ctx, name):
        self.nc, self.ctx, self.name = nc, ctx, name

    def sb(self, name, shape, dt=F32):
        return self.ctx.enter_context(self.nc.sbuf_tensor(f"{self.name}_{name}", shape, dt))

    def ps(self, name, shape=(P, BANK), dt=F32):
        return self.ctx.enter_context(self.nc.psum_tensor(f"{self.name}_{name}", list(shape), dt))

    def sem(self, name):
        return self.ctx.enter_context(self.nc.semaphore(f"{self.name}_{name}"))

    def block(self):
        return self.ctx.enter_context(self.nc.Block())


def make_ident(pool, ident, zeroed, ready):
    pool.memset(ident[:, :], 0.0).then_inc(zeroed, 1)
    pool.wait_ge(zeroed, 1)
    pool.affine_select(out=ident[:, :], in_=ident[:, :], compare_op=ALU.not_equal, fill=1.0,
                       base=0, pattern=[[-1, P]], channel_multiplier=1).then_inc(ready, 1)


def transpose_x(nc, z, x, xT_dram):
    B, N, C, KC, T = z.B, z.N, z.C, z.KC, z.T
    RING = 4
    with ExitStack() as ctx:
        s = Stage(nc, ctx, "tx")
        xin = s.sb("xin", [P, RING, C])
        xT = s.sb("xT", [P, 2, KC, RING * P])
        ident = s.sb("ident", [P, P])
        bank = [s.ps(f"bank{i}") for i in range(RING)]
        in_x = [s.sem(f"in_x{i}") for i in range(RING)]
        ident0, ident_ready = s.sem("ident0"), s.sem("ident_ready")
        mm, copied = s.sem("mm"), s.sem("copied")
        out_x = [s.sem(f"out_x{i}") for i in range(2)]
        block = s.block()
        PAIRS = B * T // RING // 2
        x_rows = x.rearrange("b n c -> (b n) c")
        out_v = xT_dram.rearrange("b (k p) n -> b p k n", p=P)

        @block.gpsimd
        def _(pool):
            pool.memset(ident[:, :], 0.0).then_inc(ident0, 1)
            pool.wait_ge(ident0, 1)
            pool.affine_select(out=ident[:, :], in_=ident[:, :], compare_op=ALU.not_equal, fill=1.0,
                               base=0, pattern=[[-1, P]], channel_multiplier=1).then_inc(ident_ready, 1)

        @block.sync
        def _(sp):
            with sp.Fori(0, PAIRS) as i:
                for h in range(2):
                    for t in range(RING):
                        sp.wait_ge(mm, (i * 2 + h) * RING if t == 0 else (i * 2 + h) * RING)
                        sp.dma_start(xin[:, t, :], x_rows[bass.ds(((i * 2 + h) * RING + t) * P, P), :]).then_inc(in_x[t], 16)

        @block.tensor
        def _(pe):
            pe.wait_ge(ident_ready, 1)
            with pe.Fori(0, PAIRS) as i:
                for h in range(2):
                    for t in range(RING):
                        pe.wait_ge(in_x[t], (i * 2 + h + 1) * 16)
                        pe.wait_ge(copied, (i * 2 + h) * RING)
                        for k in range(KC):
                            last = pe.transpose(bank[t][:, k * P:(k + 1) * P], xin[:, t, k * P:(k + 1) * P], ident[:, :])
                        last.then_inc(mm, 1)

        @block.vector
        def _(dve):
            with dve.Fori(0, PAIRS) as i:
                for h in range(2):
                    dve.wait_ge(out_x[h], i * 16)
                    for t in range(RING):
                        dve.wait_ge(mm, (i * 2 + h) * RING + t + 1)
                        dve.tensor_copy(xT[:, h, :, t * P:(t + 1) * P],
                                        bank[t][:, :].rearrange("p (k q) -> p k q", k=KC)).then_inc(copied, 1)

        @block.scalar
        def _(act):
            per_b = T // RING
            with act.Fori(0, PAIRS) as i:
                for h in range(2):
                    u = act.snap(i * 2 + h)
                    act.wait_ge(copied, (u + 1) * RING)
                    dst = out_v[bass.ds(u // per_b, 1), :, :, bass.ds(u % per_b * BANK, BANK)]
                    act.dma_start(dst.rearrange("o p k n -> (o p) k n"), xT[:, h, :, :]).then_inc(out_x[h], 16)
            for h in range(2):
                act.wait_ge(out_x[h], PAIRS * 16)


def self_attention(nc, z, xT_dram, qkv_w, qkv_b, attnT_dram):
    B, N, C, KC, G, HG, D, T, NQ = z.B, z.N, z.C, z.KC, z.G, z.HG, z.D, z.T, z.NQ
    SCALE = float(D) ** -0.5
    UNITS = B * G
    QK = 3 * D
    AUG = QK + 2
    KQ = N // BANK
    TQ = BANK // P
    NMAX = TQ * HG * KQ
    PER_STEP = NMAX // T
    EARLY = 3
    LEAD = EARLY * PER_STEP
    OPS = [(what, n) for n in range(NQ) for what in "kqv"]
    SPLITS = [o for o in OPS if o[0] != "v"]
    OP_STEPS = (4, 6, 9, 11)
    OP_AT = {(c, kt): c * len(OP_STEPS) + i for c in range(NQ - 1) for i, kt in enumerate(OP_STEPS)}
    MOVES = 3 * HG
    STEPS = T * NQ
    SCORES = STEPS * HG
    POOL_HEADS = HG - 1
    ADDS = NQ * (T - 1)
    DEN_AT, DIVIDE_AT = 1, 6
    W_LOADS = 16 * (KC + 1)
    CONSTS = 6

    with ExitStack() as ctx:
        s = Stage(nc, ctx, "sa")
        xT = s.sb("xT", [P, 2, KC, BANK])
        w = s.sb("w", [P, KC, 3, P])
        qkb = s.sb("qkb", [P, 2, G])
        vb = s.sb("vb", [P, P])
        ident = s.sb("ident", [P, P])
        ones = s.sb("ones", [P, D])
        hilo = s.sb("hilo", [P, 2, 2, BANK], F32R)
        q_stack = s.sb("q_stack", [P, 2, HG, N], F32R)
        k_stack = s.sb("k_stack", [P, 2, HG, N], F32R)
        v = s.sb("v", [P, 2, T, P])
        prob = s.sb("prob", [P, 2, HG, BANK])
        part_max = s.sb("part_max", [P, TQ, HG, KQ])
        top = s.sb("top", [P, TQ, HG])
        shift = s.sb("shift", [P, TQ, HG, 2], F32R)
        shiftT = s.sb("shiftT", [2 * HG, BANK], F32R)
        acc = s.sb("acc", [P, HG, BANK])
        sums = s.sb("sums", [P, BANK])
        recip = s.sb("recip", [P, 2, BANK])

        sc = [s.ps(f"sc{i}") for i in range(3)]
        mxp = [s.ps(f"mx{i}") for i in range(3)]
        pv = s.ps("pv")
        misc = s.ps("misc")

        in_x = [s.sem(f"in_x{i}") for i in range(2)]
        in_w, in_b = s.sem("in_w"), s.sem("in_b")
        const_ready, ident0 = s.sem("const_ready"), s.sem("ident0")
        proj_mm, v_ready = s.sem("proj_mm"), s.sem("v_ready")
        hi_ready, hilo_ready = s.sem("hi_ready"), s.sem("hilo_ready")
        stacked = [s.sem(f"stacked{i}") for i in range(len(SPLITS))]
        max_mm, max_read = s.sem("max_mm"), s.sem("max_read")
        top_ready, shift_hi, shift_ready = s.sem("top_ready"), s.sem("shift_hi"), s.sem("shift_ready")
        shift_mm, shiftT_ready, shift_in = s.sem("shift_mm"), s.sem("shiftT_ready"), s.sem("shift_in")
        sc_mm, prob_ready = s.sem("sc_mm"), s.sem("prob_ready")
        pv_mm, sums_ready, attn_ready = s.sem("pv_mm"), s.sem("sums_ready"), s.sem("attn_ready")
        acc_pool, acc_dve, den_mm, recip_ready = s.sem("acc_pool"), s.sem("acc_dve"), s.sem("den_mm"), s.sem("recip_ready")
        attn_out = [s.sem(f"attn_out{i}") for i in range(2)]
        block = s.block()

        w_v = qkv_w.rearrange("(k p) (a c) -> p k a c", p=P, a=3)
        vb_v = qkv_b[2 * C:3 * C].rearrange("(o c) -> o c", o=1)
        xT_v = xT_dram.rearrange("b (k p) n -> b p k n", p=P)

        def counts(engine, u):
            known = {}

            def at(per):
                if per not in known:
                    known[per] = engine.snap(u * per)
                return known[per]
            return at

        def zero(per):
            return 0

        @block.gpsimd
        def _(pool):
            pool.memset(ident[:, :], 0.0).then_inc(ident0, 1)
            pool.wait_ge(ident0, 1)
            pool.affine_select(out=ident[:, :], in_=ident[:, :], compare_op=ALU.not_equal, fill=1.0,
                               base=0, pattern=[[-1, P]], channel_multiplier=1).then_inc(const_ready, 1)

            def divide(at, c):
                pool.wait_ge(sums_ready, at(NQ) + c)
                pool.wait_ge(recip_ready, at(TQ * NQ) + TQ * (c + 1))
                pool.tensor_tensor(recip[:, (c + 1) % 2, :], sums[:, :], recip[:, (c + 1) % 2, :], ALU.mult).then_inc(attn_ready, 1)

            pool.sem_inc(acc_pool, 1)
            pool.wait_ge(const_ready, CONSTS)
            with pool.Fori(0, UNITS // 2) as pair:
                for p in range(2):
                    at = counts(pool, pool.snap(pair * 2 + p))
                    for c in range(NQ):
                        for kt in range(1, T):
                            pool.wait_ge(prob_ready, at(SCORES) + (c * T + kt) * HG + POOL_HEADS)
                            if kt == 1:
                                pool.wait_ge(den_mm, at(NQ) + c + 1)
                                other = prob[:, 0, 0:POOL_HEADS, :]
                            else:
                                pool.wait_ge(acc_pool, at(ADDS) + c * (T - 1) + kt)
                                other = acc[:, 0:POOL_HEADS, :]
                            pool.tensor_tensor(acc[:, 0:POOL_HEADS, :], prob[:, kt % 2, 0:POOL_HEADS, :], other, ALU.add).then_inc(acc_pool, 1)
                            if kt == DIVIDE_AT:
                                divide(at, c)
            divide(lambda per: UNITS * per, 0)

        @block.sync
        def _(sp):
            sp.dma_start(qkb[:, :, :], qkv_b[0:2 * C].rearrange("(a g p) -> p a g", a=2, p=P),
                         allow_slow_non_contiguous=True).then_inc(in_b, 16)

            def load_weights(done, g):
                sp.wait_ge(proj_mm, done(len(OPS)))
                for k in range(KC):
                    sp.dma_start(w[:, k, :, :], w_v[:, k, :, bass.ds(g * P, P)]).then_inc(in_w, 16)
                sp.wait_ge(v_ready, done(NQ))
                sp.dma_start(vb[:, :], vb_v[:, bass.ds(g * P, P)].broadcast_to([P, P])).then_inc(in_w, 16)

            def load_x(done, b, n):
                sp.wait_ge(proj_mm, done(len(OPS)) + (3 * (n - 1) if n >= 2 else 0))
                sp.dma_start(xT[:, n % 2, :, :], xT_v[bass.ds(b, 1), :, :, n * BANK:(n + 1) * BANK]
                             .rearrange("o p k n -> (o p) k n")).then_inc(in_x[n % 2], 16)

            def load_first(done, u):
                load_weights(done, u % G)
                for n in range(2):
                    load_x(done, u // G, n)

            def stream(done, i, b, buf):
                what, n = SPLITS[i]
                if what == "k" and 2 <= n + 1 < NQ:
                    load_x(done, b, n + 1)
                stack_chunk(done, i, buf)

            def stack_chunk(done, i, buf):
                what, n = SPLITS[i]
                sp.wait_ge(hilo_ready, done(len(SPLITS)) + i + 1)
                stack = q_stack if what == "q" else k_stack
                for j in range(HG):
                    for r, part in enumerate((0, 0, 1) if what == "q" else (0, 1, 0)):
                        sp.dma_start(stack[D * r:D * (r + 1), buf, j, n * BANK:(n + 1) * BANK].bitcast(F32),
                                     hilo[D * j:D * (j + 1), i % 2, part, :].bitcast(F32)).then_inc(stacked[i], 16)

            def shift_rows(n, c, buf):
                sp.wait_ge(shiftT_ready, n)
                for j in range(HG):
                    sp.dma_start(q_stack[QK:AUG, buf, j, c * BANK:(c + 1) * BANK].bitcast(F32),
                                 shiftT[2 * j:2 * j + 2, :].bitcast(F32)).then_inc(shift_in, 16)

            def store(at, c, unit):
                before = (c - 1) % NQ
                sp.wait_ge(attn_ready, at(NQ) + c + 1)
                dst = attnT_dram[bass.ds(unit // G, 1), bass.ds(unit % G * P, P), before * BANK:(before + 1) * BANK]
                sp.dma_start(dst.rearrange("o p n -> (o p) n"), recip[:, before % 2, :]).then_inc(attn_out[before % 2], 16)

            load_first(zero, 0)
            for i in range(len(SPLITS)):
                stream(zero, i, 0, 0)
            load_first(lambda per: per, 1)
            shift_rows(1, 0, 0)
            with sp.Fori(0, UNITS // 2) as pair:
                for p in range(2):
                    u = sp.snap(pair * 2 + p)
                    at = counts(sp, u)
                    b_next = sp.snap((u + 1) % UNITS // G)

                    for c in range(NQ):
                        if c + 1 == NQ:
                            load_first(lambda per: at(per) + 2 * per, sp.snap((u + 2) % UNITS))
                        for kt in range(T):
                            if kt == DIVIDE_AT + 1:
                                store(at, c, u if c else sp.snap((u + UNITS - 1) % UNITS))
                            op = OP_AT.get((c, kt))
                            if op is not None and OPS[op] in SPLITS:
                                stream(lambda per: at(per) + per, SPLITS.index(OPS[op]), b_next, 1 - p)
                        shift_rows(at(NQ) + c + 2, (c + 1) % NQ, p if c + 1 < NQ else 1 - p)
            store(lambda per: UNITS * per, 0, UNITS - 1)
            sp.wait_ge(in_w, (UNITS + 2) * W_LOADS)
            for i in range(2):
                sp.wait_ge(in_x[i], (UNITS + 1) * (NQ // 2) * 16 + 16)
            sp.wait_ge(shift_in, (UNITS * NQ + 1) * 16 * HG)
            for i in range(len(SPLITS)):
                sp.wait_ge(stacked[i], (UNITS + 1) * 16 * MOVES)
            for i in range(2):
                sp.wait_ge(attn_out[i], 16 * (UNITS * NQ // 2 + i))

        @block.scalar
        def _(act):
            with act.Fori(0, UNITS // 2) as pair:
                for p in range(2):
                    u = act.snap(pair * 2 + p)
                    at = counts(act, u)
                    for c in range(NQ):
                        for kt in range(T):
                            step = c * T + kt
                            for j in range(HG):
                                n = step * HG + j
                                act.wait_ge(sc_mm, at(SCORES) + n + 1)
                                if j == 0:
                                    act.wait_ge(pv_mm, at(STEPS) + step)
                                    adds = c * (T - 1) + (max(kt - 2, 1) if kt >= 2 else kt - 1)
                                    act.wait_ge(acc_pool, at(ADDS) + adds + 1)
                                    act.wait_ge(acc_dve, at(ADDS) + adds + 1)
                                act.activation(prob[:, kt % 2, j, :], sc[n % 3][:, :], ACT.Exp, scale=SCALE).then_inc(prob_ready, 1)
                        act.wait_ge(pv_mm, at(STEPS) + (c + 1) * T + 1)
                        act.wait_ge(attn_ready, at(NQ) + c + 1)
                        act.activation(sums[:, :], pv[:, :], ACT.Copy).then_inc(sums_ready, 1)

        @block.vector
        def _(dve):
            dve.memset(ones[:, :], 1.0).then_inc(const_ready, 1)
            dve.memset(k_stack[QK:AUG, :, :, :].bitcast(F32), 1.0).then_inc(const_ready, 1)
            for constant in (acc[:, :, :], sums[:, :], prob[:, 1, HG - 1, :]):
                dve.memset(constant, 1.0).then_inc(const_ready, 1)
            dve.wait_ge(in_b, 16)

            def leave_psum(done, o, g, buf):
                what, n = OPS[o]
                dve.wait_ge(proj_mm, done(len(OPS)) + o + 1)
                if what == "v":
                    dve.wait_ge(in_w, done(W_LOADS) + W_LOADS)
                    bias = vb[:, :].rearrange("p (o c) -> p o c", o=1).broadcast_to([P, TQ, P])
                    dve.tensor_tensor(v[:, buf, n * TQ:(n + 1) * TQ, :], misc[:, :].rearrange("p (t c) -> p t c", t=TQ),
                                      bias, ALU.add).then_inc(v_ready, 1)
                    return
                i = SPLITS.index(OPS[o])
                bias = qkb[:, 0 if what == "q" else 1, bass.ds(g, 1)]
                dve.wait_ge(stacked[i - 2], done(16 * MOVES) + (16 * MOVES if i >= 2 else 0))
                dve.tensor_scalar(hilo[:, i % 2, 0, :], misc[:, :], bias, None, ALU.add).then_inc(hi_ready, 1)
                dve.wait_ge(hi_ready, done(len(SPLITS)) + i + 1)
                dve.scalar_tensor_tensor(out=hilo[:, i % 2, 1, :], in0=misc[:, :], scalar=bias,
                                         in1=hilo[:, i % 2, 0, :].bitcast(F32), op0=ALU.add, op1=ALU.subtract).then_inc(hilo_ready, 1)

            def reduce_max(n, m, bank):
                dve.wait_ge(max_mm, n + 1)
                q, j, k = m // (HG * KQ), m // KQ % HG, m % KQ
                dve.reduce_max(part_max[:, q, j, k:k + 1], mxp[bank % 3][:, :], AX_X).then_inc(max_read, 1)

            def make_shift(reads, n):
                dve.wait_ge(max_read, reads)
                dve.reduce_max(top[:, :, :], part_max[:, :, :, :], AX_X).then_inc(top_ready, 1)
                dve.wait_ge(shift_mm, n)
                dve.wait_ge(top_ready, n + 1)
                dve.tensor_scalar(shift[:, :, :, 0], top[:, :, :], -1.0, None, ALU.mult).then_inc(shift_hi, 1)
                dve.wait_ge(shift_hi, n + 1)
                dve.scalar_tensor_tensor(out=shift[:, :, :, 1], in0=top[:, :, :], scalar=-1.0,
                                         in1=shift[:, :, :, 0].bitcast(F32), op0=ALU.mult, op1=ALU.subtract).then_inc(shift_ready, 1)

            def leave_shift(n, ins):
                dve.wait_ge(shift_mm, n + 1)
                dve.wait_ge(shift_in, ins)
                dve.tensor_copy(shiftT[:, :], misc[0:2 * HG, :]).then_inc(shiftT_ready, 1)

            for o in range(len(OPS)):
                leave_psum(zero, o, 0, 0)
            for m in range(NMAX):
                reduce_max(m, m, m)
            make_shift(NMAX, 0)
            leave_shift(0, 0)
            for m in range(LEAD):
                reduce_max(NMAX + m, m, NMAX + m)
            def add_last_head(at, c, kt):
                dve.wait_ge(prob_ready, at(SCORES) + (c * T + kt + 1) * HG)
                if kt == 1:
                    dve.wait_ge(den_mm, at(NQ) + c + 1)
                    other = prob[:, 0, HG - 1, :]
                else:
                    dve.wait_ge(acc_dve, at(ADDS) + c * (T - 1) + kt)
                    other = acc[:, HG - 1, :]
                dve.tensor_tensor(acc[:, HG - 1, :], prob[:, kt % 2, HG - 1, :], other, ALU.add).then_inc(acc_dve, 1)

            def add_last_of_chunk_before(at, c):
                dve.wait_ge(prob_ready, at(SCORES) + c * (T * HG))
                dve.wait_ge(acc_dve, at(ADDS) + c * (T - 1))
                dve.tensor_tensor(acc[:, HG - 1, :], prob[:, 1, HG - 1, :], acc[:, HG - 1, :], ALU.add).then_inc(acc_dve, 1)

            def invert(at, c, q):
                if q == 0:
                    dve.wait_ge(den_mm, at(NQ) + c + 1)
                    dve.wait_ge(attn_out[(c + 1) % 2], at(NQ // 2 * 16) + c // 2 * 16)
                dve.reciprocal(recip[:, (c + 1) % 2, q * P:(q + 1) * P], misc[:, q * P:(q + 1) * P]).then_inc(recip_ready, 1)

            with dve.Fori(0, UNITS // 2) as pair:
                for p in range(2):
                    u = dve.snap(pair * 2 + p)
                    at = counts(dve, u)
                    g_next = dve.snap((u + 1) % G)
                    for c in range(NQ):
                        for kt in range(T):
                            for i in range(PER_STEP):
                                m = LEAD + kt * PER_STEP + i
                                reduce_max(at(NQ * NMAX) + (c + 1) * NMAX + m, m % NMAX, c * NMAX + m - LEAD)
                                if i == 0 and kt == T - EARLY + 1:
                                    leave_shift(at(NQ) + c + 1, at(NQ * 16 * HG) + (c + 1) * 16 * HG)
                                if i == 1 and (c, kt - 1) in OP_AT:
                                    leave_psum(lambda per: at(per) + per, OP_AT[(c, kt - 1)], g_next, 1 - p)
                                if i == 2 and kt >= 2:
                                    add_last_head(at, c, kt - 1)
                                if i == 2 and kt == 0:
                                    add_last_of_chunk_before(at, c)
                                if kt == DEN_AT + 1:
                                    invert(at, c, i)
                            if kt == T - EARLY - 1:
                                make_shift(at(NQ * NMAX) + (c + 2) * NMAX, at(NQ) + c + 1)
            after = lambda per: UNITS * per
            add_last_of_chunk_before(after, 0)
            for q in range(TQ):
                invert(after, 0, q)

        @block.tensor
        def _(pe):
            pe.wait_ge(const_ready, CONSTS)
            pe.sem_inc(pv_mm, 1)

            def project(done, o, part, inverted=None):
                what, n = OPS[o]
                if part == 0:
                    if o == 0:
                        pe.wait_ge(in_w, done(W_LOADS) + W_LOADS)
                    if o % 3 == 0:
                        pe.wait_ge(in_x[n % 2], done(NQ // 2 * 16) + (n // 2 + 1) * 16)
                    if inverted is not None:
                        pe.wait_ge(recip_ready, inverted)
                    if o:
                        if OPS[o - 1] in SPLITS:
                            pe.wait_ge(hilo_ready, done(len(SPLITS)) + SPLITS.index(OPS[o - 1]) + 1)
                        else:
                            pe.wait_ge(v_ready, done(NQ) + OPS[o - 1][1] + 1)
                if what == "v":
                    for k in range(KC):
                        last = pe.matmul(misc[:, part * P:(part + 1) * P], xT[:, n % 2, k, part * P:(part + 1) * P], w[:, k, 2, :],
                                         start=(k == 0), stop=(k == KC - 1))
                else:
                    last = pe.matmul(misc[:, :], w[:, part, 0 if what == "q" else 1, :], xT[:, n % 2, part, :],
                                     start=(part == 0), stop=(part == KC - 1))
                if part == KC - 1:
                    last.then_inc(proj_mm, 1)

            def max_pass(n, m, bank, c, buf, first=False):
                if bank >= 3:
                    pe.wait_ge(max_read, n - 2)
                elif not first:
                    pe.wait_ge(max_read, n)
                q, j, k = m // (HG * KQ), m // KQ % HG, m % KQ
                at = c * BANK + q * P
                pe.matmul(mxp[bank % 3][:, :], q_stack[0:QK, buf, j, at:at + P], k_stack[0:QK, buf, j, k * BANK:(k + 1) * BANK],
                          start=True, stop=True).then_inc(max_mm, 1)

            def transpose_shift(n):
                pe.wait_ge(shift_ready, n + 1)
                for q in range(TQ):
                    last = pe.transpose(misc[0:2 * HG, q * P:(q + 1) * P],
                                        shift[:, q, :, :].bitcast(F32).rearrange("p j a -> p (j a)"), ident[:, :])
                last.then_inc(shift_mm, 1)

            for o in range(len(OPS)):
                for part in range(KC):
                    project(zero, o, part)
            for i in range(len(SPLITS)):
                if SPLITS[i] in (("q", 0), ("q", 1)) or SPLITS[i][0] == "k":
                    pe.wait_ge(stacked[i], 16 * MOVES)
            for m in range(NMAX):
                max_pass(m, m, m, 0, 0, first=True)
            transpose_shift(0)
            for m in range(LEAD):
                max_pass(NMAX + m, m, NMAX + m, 1, 0)

            def row_sums(at, c):
                pe.wait_ge(acc_pool, at(ADDS) + c * (T - 1) + 1)
                pe.wait_ge(acc_dve, at(ADDS) + c * (T - 1) + 1)
                for j in range(HG):
                    last = pe.matmul(misc[D * j:D * (j + 1), :], ones[:, :], acc[:, j, :], start=True, stop=True)
                last.then_inc(den_mm, 1)

            with pe.Fori(0, UNITS // 2) as pair:
                for p in range(2):
                    u = pe.snap(pair * 2 + p)
                    at = counts(pe, u)

                    def add_values(c, kt, heads):
                        if 0 in heads:
                            pe.wait_ge(prob_ready, at(SCORES) + (c * T + kt + 1) * HG)
                            if kt == 0:
                                if c == 0:
                                    pe.wait_ge(v_ready, at(NQ) + NQ)
                                pe.wait_ge(sums_ready, at(NQ) + c)
                        for j in heads:
                            last = pe.matmul(pv[D * j:D * (j + 1), :], v[:, p, kt, D * j:D * (j + 1)], prob[:, kt % 2, j, :],
                                             start=(kt == 0), stop=(kt == T - 1))
                        if HG - 1 in heads:
                            last.then_inc(pv_mm, 1)

                    def score(c, kt, j):
                        n = (c * T + kt) * HG + j
                        pe.wait_ge(prob_ready, at(SCORES) + n - 2 if n >= 3 else at(SCORES))
                        pe.matmul(sc[n % 3][:, :], k_stack[0:AUG, p, j, kt * P:(kt + 1) * P],
                                  q_stack[0:AUG, p, j, c * BANK:(c + 1) * BANK], start=True, stop=True).then_inc(sc_mm, 1)

                    for c in range(NQ):
                        pe.wait_ge(shift_in, at(NQ * 16 * HG) + (c + 1) * 16 * HG)
                        for kt in range(T):
                            if kt == T - EARLY:
                                if c + 2 < NQ:
                                    pe.wait_ge(stacked[SPLITS.index(("q", c + 2))], at(16 * MOVES) + 16 * MOVES)
                                elif c + 2 == NQ:
                                    for i in range(len(SPLITS)):
                                        if SPLITS[i] == ("q", 0) or SPLITS[i][0] == "k":
                                            pe.wait_ge(stacked[i], at(16 * MOVES) + 2 * 16 * MOVES)
                                else:
                                    pe.wait_ge(stacked[SPLITS.index(("q", 1))], at(16 * MOVES) + 2 * 16 * MOVES)
                            for i in range(HG):
                                m = LEAD + kt * PER_STEP + i
                                chunk = c + 1 + m // NMAX
                                max_pass(at(NQ * NMAX) + (c + 1) * NMAX + m, m % NMAX, c * NMAX + m - LEAD, chunk % NQ, p if chunk < NQ else 1 - p)
                                score(c, kt, i)
                                if (c, kt) in OP_AT:
                                    project(lambda per: at(per) + per, OP_AT[(c, kt)], i,
                                            at(TQ * NQ) + TQ * (c + 1) if kt == OP_STEPS[0] else None)
                                if i % 2 and kt >= 1:
                                    add_values(c, kt - 1, range(i // 2 * (HG // 2), (i // 2 + 1) * (HG // 2)))
                                if i == 2 and kt == T - EARLY:
                                    transpose_shift(at(NQ) + c + 1)
                            if kt == DEN_AT:
                                row_sums(at, c)
                        add_values(c, T - 1, range(HG))
            row_sums(lambda per: UNITS * per, 0)


def cross_attention(nc, z, a):
    B, N, C, KC, M, E = z.B, z.N, z.C, z.KC, z.M, z.E
    XH, XD = z.XH, z.XD
    TQ = BANK // P
    NCH = z.TOK // BANK
    PER_B = N // BANK
    SCALE = float(XD) ** -0.5
    PAIR_M = 2 * M
    HP = XH // 2
    PER_BANK = 2
    EPS = 1e-5

    with ExitStack() as ctx:
        s = Stage(nc, ctx, "ca")
        wp, wq, wo = (s.sb(n, [P, KC, C]) for n in ("wp", "wq", "wo"))
        rw = s.sb("rw", [P, KC, E])
        rw_rows = s.sb("rw_rows", [E, C])
        pb, ob = s.sb("pb", [P, C]), s.sb("ob", [P, C])
        gl, bl, gx, bx = (s.sb(n, [P, KC]) for n in ("gl", "bl", "gx", "bx"))
        ident = s.sb("ident", [P, P])
        minus_half = s.sb("minus_half", [P, TQ])
        cin = s.sb("cin", [M, B, C])
        cmv = s.sb("cmv", [M, B, 2])
        cstat = s.sb("cstat", [M, B, 6])
        crstd = s.sb("crstd", [M, B, 1])
        cnT = s.sb("cnT", [P, KC, B, M])
        k_all = s.sb("k_all", [P, B, HP, PAIR_M])
        v_all = s.sb("v_all", [M, B, C])
        wkv = s.sb("wkv", [P, KC, C])
        k_cur = s.sb("k_cur", [P, HP, PAIR_M])
        v_cur = s.sb("v_cur", [M, C])

        aT = s.sb("aT", [P, 2, KC, BANK])
        xb = s.sb("xb", [P, TQ, C])
        r1 = s.sb("r1", [P, TQ, C])
        x1 = s.sb("x1", [P, 2, TQ, C])
        x1n = s.sb("x1n", [P, TQ, C])
        x1b = s.sb("x1b", [P, TQ, C])
        x1nT = s.sb("x1nT", [P, KC, BANK])
        qT = s.sb("qT", [P, HP, BANK])
        e_in = s.sb("e_in", [P, TQ, XH, M])
        prob = e_in
        pT = s.sb("pT", [M, XH, BANK])
        oT = s.sb("oT", [P, HP, BANK])
        r2 = s.sb("r2", [P, TQ, C])
        x2 = s.sb("x2", [P, TQ, C])
        x2T = s.sb("x2T", [P, KC, BANK])
        stat = s.sb("stat", [P, 3, TQ, 6])
        mv = s.sb("mv", [P, 3, TQ, 2])
        var_eps = s.sb("var_eps", [P, 3, TQ])
        rstd = s.sb("rstd", [P, 3, TQ])
        top = s.sb("top", [P, TQ, XH])
        total = s.sb("total", [P, TQ, XH])
        inv = s.sb("inv", [P, TQ, XH])

        bank = [s.ps(f"bank{i}") for i in range(8)]

        in_c, in_w, waited = s.sem("in_c"), s.sem("in_w"), s.sem("waited")
        in_wk, in_wv = s.sem("in_wk"), s.sem("in_wv")
        id0, idr = s.sem("id0"), s.sem("idr")
        pool_c, dve_c, act_c, pe_c = s.sem("pool_c"), s.sem("dve_c"), s.sem("act_c"), s.sem("pe_c")
        in_a = [s.sem(f"in_a{i}") for i in range(2)]
        in_x, out_x2 = s.sem("in_x"), s.sem("out_x2")
        mm1, mm2t, mm2, mm3, mm4t, mm4v, mm4, mm5t, mm5 = (
            s.sem(f"mm{i}") for i in ("1", "2t", "2", "3", "4t", "4v", "4", "5t", "5"))
        xb_ready, r1_ready, x1_ready, x1b_ready, x1n_ready, x1nT_ready, qT_ready = (
            s.sem(i) for i in ("xb_ready", "r1_ready", "x1_ready", "x1b_ready", "x1n_ready", "x1nT_ready", "qT_ready"))
        stat_ready, mv_ready, ve_ready, rstd_ready = (s.sem(i) for i in ("stat_ready", "mv_ready", "ve_ready", "rstd_ready"))
        kv_cur, top_ready, e_ready, exp_ready, total_ready, inv_ready, prob_ready = (
            s.sem(i) for i in ("kv_cur", "top_ready", "e_ready", "exp_ready", "total_ready", "inv_ready", "prob_ready"))
        pT_ready, oT_ready, r2_ready, x2_ready, x2T_ready, lg_ready = (
            s.sem(i) for i in ("pT_ready", "oT_ready", "r2_ready", "x2_ready", "x2T_ready", "lg_ready"))
        block = s.block()

        x_rows = a.x.rearrange("b n c -> (b n) c")
        aT_v = a.attnT.rearrange("b (k p) n -> b p k n", p=P)
        x2_rows = a.x2

        def col(v):
            return v.rearrange("(k p) -> p k", p=P)

        def over(v):
            return v.rearrange("(o c) -> o c", o=1).broadcast_to([P, C])

        def w_tiles(w):
            return w.rearrange("(k p) c -> p k c", p=P)

        @block.sync
        def _(sp):
            sp.dma_start(cin[:, :, :], a.ctx.rearrange("b m c -> m b c")).then_inc(in_c, 16)
            for dst, src in ((gx, a.gx), (bx, a.bx), (gl, a.gl), (bl, a.bl)):
                sp.dma_start(dst[:, :], col(src), allow_slow_non_contiguous=True).then_inc(in_c, 16)
            sp.dma_start(rw_rows[:, :], a.rw).then_inc(in_c, 16)
            sp.dma_start(wkv[:, :, :], w_tiles(a.Wk)).then_inc(in_wk, 16)
            sp.dma_start(pb[:, :], over(a.proj_b)).then_inc(in_w, 16)
            sp.dma_start(ob[:, :], over(a.bo)).then_inc(in_w, 16)
            for dst, src in ((wp, a.proj_w), (wq, a.Wq), (wo, a.Wo)):
                sp.dma_start(dst[:, :, :], w_tiles(src)).then_inc(in_w, 16)
            sp.wait_ge(pe_c, 2)
            sp.dma_start(wkv[:, :, :], w_tiles(a.Wv)).then_inc(in_wv, 16)

            def load(n, ch, par):
                sp.wait_ge(mm1, n * TQ)
                sp.dma_start(aT[:, par, :, :], aT_v[bass.ds(ch // PER_B, 1), :, :, bass.ds(ch % PER_B * BANK, BANK)]
                             .rearrange("o p k n -> (o p) k n")).then_inc(in_a[par], 16)
                sp.wait_ge(r1_ready, n * TQ)
                sp.dma_start(xb[:, :, :], x_rows[bass.ds(ch * BANK, BANK), :].rearrange("(t p) c -> p t c", p=P)).then_inc(in_x, 16)

            load(0, 0, 0)
            with sp.Fori(0, NCH // 2) as i:
                for par in range(2):
                    n = sp.snap(i * 2 + par)
                    nxt = sp.snap((n + 1) % NCH)
                    load(n + 1, nxt, 1 - par)
                    sp.wait_ge(x2_ready, (n + 1) * TQ)
                    sp.dma_start(x2_rows[bass.ds(n * BANK, BANK), :].rearrange("(t p) c -> p t c", p=P), x2[:, :, :]).then_inc(out_x2, 16)
            sp.wait_ge(out_x2, NCH * 16)

        @block.gpsimd
        def _(pool):
            pool.memset(ident[:, :], 0.0).then_inc(id0, 1)
            pool.wait_ge(id0, 1)
            pool.affine_select(out=ident[:, :], in_=ident[:, :], compare_op=ALU.not_equal, fill=1.0,
                               base=0, pattern=[[-1, P]], channel_multiplier=1).then_inc(idr, 1)
            pool.wait_ge(idr, 1)
            pool.memset(minus_half[:, :], -0.5).then_inc(pool_c, 1)
            pool.wait_ge(pool_c, 1)
            pool.wait_ge(dve_c, 4)
            pool.tensor_tensor(crstd[:, :, 0], cmv[:, :, 1], minus_half[0:M, 0:B], ALU.pow).then_inc(pool_c, 1)

            def rstds(which, k):
                pool.wait_ge(ve_ready, k + 1)
                pool.tensor_tensor(rstd[:, which, :], var_eps[:, which, :], minus_half[:, :], ALU.pow).then_inc(rstd_ready, 1)

            def add_bias1(n):
                pool.wait_ge(in_x, (n + 1) * 16)
                pool.tensor_tensor(xb[:, :, :], xb[:, :, :], pb[:, :].rearrange("p (o c) -> p o c", o=1).broadcast_to([P, TQ, C]), ALU.add).then_inc(xb_ready, 1)

            pool.wait_ge(in_w, 5 * 16)
            add_bias1(0)
            rstds(0, 0)
            rstds(1, 1)
            pool.wait_ge(act_c, 2)
            with pool.Fori(0, NCH // 2) as i:
                for par in range(2):
                    n = pool.snap(i * 2 + par)
                    b = pool.snap(n // PER_B)
                    pool.wait_ge(mm3, n * TQ)
                    pool.tensor_copy(k_cur[:, :, :], k_all[:, bass.ds(b, 1), :, :].rearrange("p o h m -> p (o h) m")).then_inc(kv_cur, 1)
                    pool.wait_ge(mm4v, n)
                    pool.wait_ge(kv_cur, 2 * n + 1)
                    pool.tensor_copy(v_cur[:, :], v_all[:, bass.ds(b, 1), :].rearrange("p o c -> p (o c)")).then_inc(kv_cur, 1)
                    pool.wait_ge(kv_cur, 2 * n + 2)
                    pool.wait_ge(x1_ready, (n + 1) * TQ)
                    pool.wait_ge(r2_ready, n * TQ)
                    pool.tensor_tensor(x1b[:, :, :], x1[:, par, :, :], ob[:, :].rearrange("p (o c) -> p o c", o=1).broadcast_to([P, TQ, C]), ALU.add).then_inc(x1b_ready, 1)
                    add_bias1(n + 1)
                    rstds(0, 3 * n + 2)
                    rstds(1, 3 * n + 3)
                    rstds(2, 3 * n + 4)

        @block.vector
        def _(dve):
            dve.memset(k_all[:, :, :, :], 0.0).then_inc(dve_c, 1)
            dve.wait_ge(in_c, 6 * 16)
            for b in range(B):
                dve.bn_stats(cstat[:, b, :], cin[:, b, :]).then_inc(dve_c, 1)
            dve.wait_ge(dve_c, 1 + B)
            dve.bn_aggr(cmv[:, 0, :], cstat[:, 0, :])
            dve.bn_aggr(cmv[:, 1, :], cstat[:, 1, :]).then_inc(mv_ready, 1)
            dve.wait_ge(mv_ready, 1)
            dve.tensor_scalar(cmv[:, :, 1], cmv[:, :, 1], EPS, None, ALU.add).then_inc(dve_c, 1)
            dve.wait_ge(pool_c, 2)
            for b in range(B):
                dve.tensor_scalar(cin[:, b, :], cin[:, b, :], cmv[:, b, 0:1], crstd[:, b, :], ALU.subtract, ALU.mult).then_inc(dve_c, 1)
            dve.wait_ge(pe_c, 1)
            for k in range(KC):
                dve.tensor_scalar(cnT[:, k, :, :], bank[k][:, 0:B * M].rearrange("p (b m) -> p b m", b=B),
                                  gx[:, k:k + 1], bx[:, k:k + 1], ALU.mult, ALU.add).then_inc(dve_c, 1)
            for k in range(KC):
                last = dve.tensor_copy(rw[:, k, :], bank[4][:, k * E:(k + 1) * E])
            last.then_inc(dve_c, 1)

            def stats(which, t, src, seq):
                dve.bn_stats(stat[:, which, t, :], src).then_inc(stat_ready, 1)
                wait_alone(dve, stat_ready, seq + 1, waited)
                dve.bn_aggr(mv[:, which, t, :], stat[:, which, t, :]).then_inc(mv_ready, 1)

            def var_plus_eps(which, k):
                dve.wait_ge(mv_ready, 1 + (k + 1) * TQ)
                dve.tensor_scalar(var_eps[:, which, :], mv[:, which, :, 1], EPS, None, ALU.add).then_inc(ve_ready, 1)
                dve.wait_ge(rstd_ready, k + 1)

            def step1(n, par, k):
                dve.wait_ge(xb_ready, n + 1)
                for t in range(TQ):
                    dve.wait_ge(mm1, n * TQ + t + 1)
                    dve.tensor_tensor(r1[:, t, :], bank[t % 2][:, :], xb[:, t, :], ALU.add).then_inc(r1_ready, 1)
                    dve.wait_ge(r1_ready, n * TQ + t + 1)
                    stats(0, t, r1[:, t, :], k * TQ + t)
                var_plus_eps(0, k)
                for t in range(TQ):
                    dve.tensor_scalar(x1[:, par, t, :], r1[:, t, :], mv[:, 0, t, 0:1], rstd[:, 0, t:t + 1], ALU.subtract, ALU.mult).then_inc(x1_ready, 1)
                for t in range(TQ):
                    dve.wait_ge(x1_ready, n * TQ + t + 1)
                    stats(1, t, x1[:, par, t, :], (k + 1) * TQ + t)
                var_plus_eps(1, k + 1)
                for t in range(TQ):
                    if t == 0:
                        dve.wait_ge(mm2t, n * KC)
                    dve.tensor_scalar(x1n[:, t, :], x1[:, par, t, :], mv[:, 1, t, 0:1], rstd[:, 1, t:t + 1], ALU.subtract, ALU.mult).then_inc(x1n_ready, 1)

            def step2(n):
                for k in range(KC):
                    dve.wait_ge(mm2t, n * KC + k + 1)
                    if k == 0:
                        dve.wait_ge(mm2, n * HP)
                    dve.tensor_scalar(x1nT[:, k, :], bank[k][:, :], gl[:, k:k + 1], bl[:, k:k + 1], ALU.mult, ALU.add).then_inc(x1nT_ready, 1)

            step1(0, 0, 0)
            step2(0)
            with dve.Fori(0, NCH // 2) as i:
                for par in range(2):
                    n = dve.snap(i * 2 + par)
                    for t in range(TQ):
                        dve.wait_ge(mm3, n * TQ + t + 1)
                        for h in range(2):
                            src = bank[2 * (t % 2) + h][:, 0:PER_BANK * PAIR_M].rearrange("p (h m) -> p h m", m=M)
                            dve.reduce_max(top[:, t, 4 * h:4 * h + 4], src, AX_X).then_inc(top_ready, 1)
                        dve.wait_ge(top_ready, (n * TQ + t + 1) * 2)
                        for h in range(2):
                            src = bank[2 * (t % 2) + h][:, 0:PER_BANK * PAIR_M].rearrange("p (h m) -> p h m", m=M)
                            sub = top[:, t, 4 * h:4 * h + 4].rearrange("p (h o) -> p h o", o=1).broadcast_to([P, 4, M])
                            dve.tensor_tensor(e_in[:, t, 4 * h:4 * h + 4, :], src, sub, ALU.subtract).then_inc(e_ready, 1)
                    for t in range(TQ):
                        dve.wait_ge(exp_ready, n * TQ + t + 1)
                        dve.reduce_sum(total[:, t, :], e_in[:, t, :, :], AX_X).then_inc(total_ready, 1)
                    dve.wait_ge(total_ready, (n + 1) * TQ)
                    dve.reciprocal(inv[:, :, :], total[:, :, :]).then_inc(inv_ready, 1)
                    dve.wait_ge(inv_ready, n + 1)
                    for t in range(TQ):
                        by = inv[:, t, :].rearrange("p (h o) -> p h o", o=1).broadcast_to([P, XH, M])
                        dve.tensor_tensor(prob[:, t, :, :], e_in[:, t, :, :], by, ALU.mult).then_inc(prob_ready, 1)
                    step1(n + 1, 1 - par, 3 * n + 2)
                    dve.wait_ge(x1b_ready, n + 1)
                    for t in range(TQ):
                        dve.wait_ge(mm4, n * TQ + t + 1)
                        dve.tensor_tensor(r2[:, t, :], bank[4 + t % 2][:, :], x1b[:, t, :], ALU.add).then_inc(r2_ready, 1)
                        dve.wait_ge(r2_ready, n * TQ + t + 1)
                        stats(2, t, r2[:, t, :], (3 * n + 4) * TQ + t)
                    step2(n + 1)
                    var_plus_eps(2, 3 * n + 4)
                    dve.wait_ge(out_x2, n * 16)
                    dve.wait_ge(mm5t, n * KC)
                    for t in range(TQ):
                        dve.tensor_scalar(x2[:, t, :], r2[:, t, :], mv[:, 2, t, 0:1], rstd[:, 2, t:t + 1], ALU.subtract, ALU.mult).then_inc(x2_ready, 1)
                    dve.wait_ge(mm5, n + 1)
                    dve.tensor_copy(a.logits[:, bass.ds(n * TQ, TQ), :], bank[7][:, 0:TQ * E].rearrange("p (t e) -> p t e", e=E)).then_inc(lg_ready, 1)

        @block.scalar
        def _(act):
            act.wait_ge(pe_c, 2)
            act.wait_ge(dve_c, 1)
            for h in range(HP):
                for half in range(2):
                    rows = slice(half * XD, (half + 1) * XD)
                    last = act.activation(k_all[rows, :, h, half * M:(half + 1) * M],
                                          bank[h][rows, 0:B * M].rearrange("p (b m) -> p b m", b=B), ACT.Copy)
            last.then_inc(act_c, 1)
            act.wait_ge(pe_c, 3)
            for b in range(B):
                last = act.activation(v_all[:, b, :], bank[4 + b][0:M, :], ACT.Copy)
            last.then_inc(act_c, 1)

            def q_out(n):
                for h in range(HP):
                    act.wait_ge(mm2, n * HP + h + 1)
                    if h == 0:
                        act.wait_ge(mm3, n * TQ)
                    act.activation(qT[:, h, :], bank[4 + h % 2][:, :], ACT.Copy).then_inc(qT_ready, 1)

            q_out(0)
            with act.Fori(0, NCH // 2) as i:
                for par in range(2):
                    n = act.snap(i * 2 + par)
                    for t in range(TQ):
                        act.wait_ge(e_ready, (n * TQ + t + 1) * 2)
                        act.activation(e_in[:, t, :, :], e_in[:, t, :, :], ACT.Exp, scale=SCALE).then_inc(exp_ready, 1)
                    for t in range(TQ):
                        act.wait_ge(mm4t, n * TQ + t + 1)
                        if t == 0:
                            act.wait_ge(mm4v, n)
                        for h in range(2):
                            act.activation(pT[:, 4 * h:4 * h + 4, t * P:(t + 1) * P],
                                           bank[2 + 2 * (t % 2) + h][0:M, :].rearrange("m (h q) -> m h q", h=4), ACT.Copy).then_inc(pT_ready, 1)
                    act.wait_ge(mm4v, n + 1)
                    act.wait_ge(mm4, n * TQ)
                    for h in range(HP):
                        act.activation(oT[:, h, :], bank[(6, 7, 2, 3)[h]][:, :], ACT.Copy).then_inc(oT_ready, 1)
                    q_out(n + 1)
                    act.wait_ge(mm5, n)
                    for k in range(KC):
                        act.wait_ge(mm5t, n * KC + k + 1)
                        act.activation(x2T[:, k, :], bank[k][:, :], ACT.Copy).then_inc(x2T_ready, 1)

        @block.tensor
        def _(pe):
            pe.wait_ge(idr, 1)
            pe.wait_ge(dve_c, 2 + B + B)
            for k in range(KC):
                for b in range(B):
                    pe.transpose(bank[k][:, b * M:(b + 1) * M], cin[:, b, k * P:(k + 1) * P], ident[0:M, 0:M])
            for k in range(KC):
                last = pe.transpose(bank[4][:, k * E:(k + 1) * E], rw_rows[:, k * P:(k + 1) * P], ident[0:E, 0:E])
            last.then_inc(pe_c, 1)
            pe.wait_ge(dve_c, 2 + 2 * B + KC + 1)
            pe.wait_ge(in_wk, 16)
            for h in range(HP):
                for k in range(KC):
                    last = pe.matmul(bank[h][:, 0:B * M], wkv[:, k, h * P:(h + 1) * P], cnT[:, k, :, :].rearrange("p b m -> p (b m)"),
                                     start=(k == 0), stop=(k == KC - 1))
            last.then_inc(pe_c, 1)
            pe.wait_ge(in_wv, 16)
            for b in range(B):
                for k in range(KC):
                    last = pe.matmul(bank[4 + b][0:M, :], cnT[:, k, b, :], wkv[:, k, :], start=(k == 0), stop=(k == KC - 1))
            last.then_inc(pe_c, 1)
            pe.wait_ge(act_c, 2)
            pe.wait_ge(in_w, 5 * 16)

            def step1(n, par):
                pe.wait_ge(in_a[par], (n // 2 + 1) * 16)
                for t in range(TQ):
                    if t >= 2:
                        pe.wait_ge(r1_ready, n * TQ + t - 1)
                    for k in range(KC):
                        last = pe.matmul(bank[t % 2][:, :], aT[:, par, k, t * P:(t + 1) * P], wp[:, k, :], start=(k == 0), stop=(k == KC - 1))
                    last.then_inc(mm1, 1)

            def step2(n):
                pe.wait_ge(x1n_ready, (n + 1) * TQ)
                for k in range(KC):
                    for t in range(TQ):
                        last = pe.transpose(bank[k][:, t * P:(t + 1) * P], x1n[:, t, k * P:(k + 1) * P], ident[:, :])
                    last.then_inc(mm2t, 1)
                pe.wait_ge(x1nT_ready, (n + 1) * KC)
                for h in range(HP):
                    if h >= 2:
                        pe.wait_ge(qT_ready, n * HP + h - 1)
                    for k in range(KC):
                        last = pe.matmul(bank[4 + h % 2][:, :], wq[:, k, h * P:(h + 1) * P], x1nT[:, k, :], start=(k == 0), stop=(k == KC - 1))
                    last.then_inc(mm2, 1)

            step1(0, 0)
            step2(0)
            with pe.Fori(0, NCH // 2) as i:
                for par in range(2):
                    n = pe.snap(i * 2 + par)
                    pe.wait_ge(qT_ready, (n + 1) * HP)
                    pe.wait_ge(kv_cur, 2 * n + 2)
                    pe.wait_ge(x2T_ready, n * KC)
                    for t in range(TQ):
                        if t >= 2:
                            pe.wait_ge(e_ready, (n * TQ + t - 1) * 2)
                        for h in range(HP):
                            last = pe.matmul(bank[2 * (t % 2) + h // 2][:, h % 2 * PAIR_M:(h % 2 + 1) * PAIR_M],
                                             qT[:, h, t * P:(t + 1) * P], k_cur[:, h, :], start=True, stop=True)
                        last.then_inc(mm3, 1)
                    pe.wait_ge(e_ready, (n + 1) * 2 * TQ)
                    step1(n + 1, 1 - par)
                    for t in range(TQ):
                        pe.wait_ge(prob_ready, n * TQ + t + 1)
                        if t >= 2:
                            pe.wait_ge(pT_ready, (n * TQ + t - 1) * 2)
                        for h in range(XH):
                            last = pe.transpose(bank[2 + 2 * (t % 2) + h // 4][0:M, h % 4 * P:(h % 4 + 1) * P], prob[:, t, h, :], ident[:, :])
                        last.then_inc(mm4t, 1)
                    pe.wait_ge(pT_ready, (n + 1) * 2 * TQ)
                    pe.wait_ge(lg_ready, n)
                    for h in range(XH):
                        half = slice(h % 2 * XD, (h % 2 + 1) * XD)
                        last = pe.matmul(bank[(6, 7, 2, 3)[h // 2]][half, :], v_cur[:, h * XD:(h + 1) * XD], pT[:, h, :], start=True, stop=True)
                    last.then_inc(mm4v, 1)
                    pe.wait_ge(oT_ready, (n + 1) * HP)
                    for t in range(TQ):
                        if t >= 2:
                            pe.wait_ge(r2_ready, n * TQ + t - 1)
                        for k in range(KC):
                            last = pe.matmul(bank[4 + t % 2][:, :], oT[:, k, t * P:(t + 1) * P], wo[:, k, :], start=(k == 0), stop=(k == KC - 1))
                        last.then_inc(mm4, 1)
                    pe.wait_ge(x1n_ready, (n + 2) * TQ)
                    for k in range(KC):
                        for t in range(TQ):
                            last = pe.transpose(bank[k][:, t * P:(t + 1) * P], x1n[:, t, k * P:(k + 1) * P], ident[:, :])
                        last.then_inc(mm2t, 1)
                    pe.wait_ge(x1nT_ready, (n + 2) * KC)
                    for h in range(HP):
                        if h < 2:
                            pe.wait_ge(r2_ready, n * TQ + 3 + h)
                        else:
                            pe.wait_ge(qT_ready, (n + 1) * HP + h - 1)
                        for k in range(KC):
                            last = pe.matmul(bank[4 + h % 2][:, :], wq[:, k, h * P:(h + 1) * P], x1nT[:, k, :], start=(k == 0), stop=(k == KC - 1))
                        last.then_inc(mm2, 1)
                    pe.wait_ge(x2_ready, (n + 1) * TQ)
                    for k in range(KC):
                        for t in range(TQ):
                            last = pe.transpose(bank[k][:, t * P:(t + 1) * P], x2[:, t, k * P:(k + 1) * P], ident[:, :])
                        last.then_inc(mm5t, 1)
                    pe.wait_ge(x2T_ready, (n + 1) * KC)
                    for t in range(TQ):
                        for k in range(KC):
                            last = pe.matmul(bank[7][:, t * E:(t + 1) * E], x2T[:, k, t * P:(t + 1) * P], rw[:, k, :], start=(k == 0), stop=(k == KC - 1))
                    last.then_inc(mm5, 1)


def route(nc, z, a):
    E, CAP, NT = z.E, z.CAP, z.TOK // P
    SLOTS = E * CAP
    ST = SLOTS // P
    SKIP = 2 ** 20

    with ExitStack() as ctx:
        s = Stage(nc, ctx, "rt")
        iota_i = s.sb("iota_i", [P, NT, E], I32)
        iota_e = s.sb("iota_e", [P, NT, E])
        token = s.sb("token", [P, NT], I32)
        ident = s.sb("ident", [P, P])
        before = s.sb("before", [P, P])
        ones = s.sb("ones", [P, P])
        top, total, best, place = (s.sb(n, [P, NT]) for n in ("top", "total", "best", "place"))
        kept, weight, slot_f, skip_f = (s.sb(n, [P, NT]) for n in ("kept", "weight", "slot_f", "skip_f"))
        skip_i = s.sb("skip_i", [P, NT], I32)
        lx, ex, hot, cand, at_tile = (s.sb(n, [P, NT, E]) for n in ("lx", "ex", "hot", "cand", "at_tile"))
        zeros = s.sb("zeros", [P, NT])
        zero_i = s.sb("zero_i", [ST, P], I32)
        rows_i = s.sb("rows_i", [ST, P], I32)
        rows_f = s.sb("rows_f", [ST, P])
        in_tile, tiles, tabT = s.ps("in_tile"), s.ps("tiles"), s.ps("tabT")

        made, step, exp_ready, mm = s.sem("made"), s.sem("step"), s.sem("exp_ready"), s.sem("mm")
        table0, scattered, table_in = s.sem("table0"), s.sem("scattered"), s.sem("table_in")
        block = s.block()
        SLOTS_KNOWN = 20 + E
        table_rows = a.table.rearrange("(r c) o -> r (c o)", c=P)

        @block.gpsimd
        def _(pool):
            done = [0]

            def then(instruction):
                instruction.then_inc(made, 1)
                done[0] += 1
                pool.wait_ge(made, done[0])

            then(pool.memset(zero_i[:, :], 0))
            pool.dma_start(table_rows, zero_i[:, :]).then_inc(table0, 16)
            then(pool.iota(iota_i[:, :, :], pattern=[[0, NT], [1, E]], base=0, channel_multiplier=0))
            then(pool.iota(token[:, :], pattern=[[P, NT]], base=0, channel_multiplier=1))
            then(pool.memset(ones[:, :], 1.0))
            then(pool.affine_select(out=before[:, :], in_=ones[:, :], compare_op=ALU.is_gt, fill=0.0,
                                    base=0, pattern=[[1, P]], channel_multiplier=-1))
            then(pool.memset(ident[:, :], 0.0))
            then(pool.affine_select(out=ident[:, :], in_=ident[:, :], compare_op=ALU.not_equal, fill=1.0,
                                    base=0, pattern=[[-1, P]], channel_multiplier=1))
            pool.wait_ge(step, SLOTS_KNOWN)
            pool.wait_ge(table0, 16)
            for t in range(NT):
                pool.indirect_dma_start(a.table, bass.IndirectOffsetOnAxis(ap=skip_i[:, t:t + 1], axis=0),
                                        token[:, t:t + 1], None, bounds_check=SLOTS - 1, oob_is_err=False).then_inc(scattered, 16)
            pool.wait_ge(scattered, 16 * NT)
            pool.dma_start(rows_i[:, :], table_rows).then_inc(table_in, 16)
            pool.wait_ge(table_in, 16)

        @block.vector
        def _(dve):
            done = [0]

            def then(instruction):
                instruction.then_inc(step, 1)
                done[0] += 1
                dve.wait_ge(step, done[0])

            def each(v):
                return v[:, :].rearrange("p (t o) -> p t o", o=1).broadcast_to([P, NT, E])

            dve.wait_ge(made, 7)
            then(dve.tensor_copy(iota_e[:, :, :], iota_i[:, :, :]))
            then(dve.memset(zeros[:, :], 0.0))
            then(dve.reduce_max(top[:, :], a.logits[:, :, :], AX_X))
            then(dve.tensor_tensor(lx[:, :, :], a.logits[:, :, :], each(top), ALU.subtract))
            then(dve.tensor_scalar(cand[:, :, :], lx[:, :, :], 0.0, float(E), ALU.is_lt, ALU.mult))
            then(dve.tensor_tensor(cand[:, :, :], cand[:, :, :], iota_e[:, :, :], ALU.add))
            then(dve.tensor_reduce(best[:, :], cand[:, :, :], AX_X, ALU.min))
            then(dve.tensor_tensor(hot[:, :, :], iota_e[:, :, :], each(best), ALU.is_equal))
            assert done[0] == 8
            dve.wait_ge(exp_ready, 1)
            then(dve.reduce_sum(total[:, :], ex[:, :, :], AX_X))
            then(dve.reciprocal(weight[:, :], total[:, :]))
            dve.wait_ge(mm, 1)
            for e in range(E):
                then(dve.tensor_tensor_scan(at_tile[:, :, e], tiles[:, 0:NT * E].rearrange("p (t e) -> p t e", e=E)[:, :, e], zeros[:, :],
                                            0.0, ALU.add, ALU.add))
            then(dve.tensor_tensor(at_tile[:, :, :], at_tile[:, :, :], tiles[:, 0:NT * E].rearrange("p (t e) -> p t e", e=E), ALU.subtract))
            then(dve.tensor_tensor(at_tile[:, :, :], at_tile[:, :, :], in_tile[:, 0:NT * E].rearrange("p (t e) -> p t e", e=E), ALU.add))
            then(dve.tensor_tensor(at_tile[:, :, :], at_tile[:, :, :], hot[:, :, :], ALU.mult))
            then(dve.reduce_sum(place[:, :], at_tile[:, :, :], AX_X))
            then(dve.tensor_scalar(kept[:, :], place[:, :], float(CAP), None, ALU.is_lt))
            then(dve.tensor_scalar(slot_f[:, :], place[:, :], float(CAP - 1), None, ALU.min))
            then(dve.scalar_tensor_tensor(out=slot_f[:, :], in0=best[:, :], scalar=float(CAP), in1=slot_f[:, :], op0=ALU.mult, op1=ALU.add))
            then(dve.tensor_scalar(skip_f[:, :], kept[:, :], -float(SKIP), float(SKIP), ALU.mult, ALU.add))
            then(dve.tensor_tensor(skip_f[:, :], skip_f[:, :], slot_f[:, :], ALU.add))
            then(dve.tensor_copy(skip_i[:, :], skip_f[:, :]))
            assert done[0] == SLOTS_KNOWN
            then(dve.tensor_copy(a.slots[:, :], slot_f[:, :]))
            then(dve.tensor_tensor(a.weights[:, :], weight[:, :], kept[:, :], ALU.mult))
            dve.wait_ge(table_in, 16)
            then(dve.tensor_copy(rows_f[:, :], rows_i[:, :]))
            dve.wait_ge(mm, 2)
            then(dve.tensor_copy(a.tokens[:, :], tabT[:, 0:ST]))

        @block.scalar
        def _(act):
            act.wait_ge(step, 4)
            act.activation(ex[:, :, :], lx[:, :, :], ACT.Exp).then_inc(exp_ready, 1)

        @block.tensor
        def _(pe):
            pe.wait_ge(made, 7)
            pe.wait_ge(step, 8)
            cols = hot[:, :, :].rearrange("p t e -> p (t e)")
            pe.matmul(in_tile[:, 0:NT * E], before[:, :], cols, start=True, stop=True)
            pe.matmul(tiles[:, 0:NT * E], ones[:, :], cols, start=True, stop=True).then_inc(mm, 1)
            pe.wait_ge(step, SLOTS_KNOWN + 3)
            pe.transpose(tabT[:, 0:ST], rows_f[:, :], ident[0:ST, 0:ST]).then_inc(mm, 1)


def experts(nc, z, a):
    E, CAP, C, KC, F = z.E, z.CAP, z.C, z.KC, z.F
    TS = CAP // P
    HALF = CAP // 2
    STEPS = F // P
    QUADS = STEPS // 4
    PARTS = ((0, 0), (0, 1), (1, 0))
    FREE = 2

    with ExitStack() as ctx:
        s = Stage(nc, ctx, "ex")
        ident = s.sb("ident", [P, P])
        b1_rows = s.sb("b1_rows", [E * STEPS, P])
        b1 = s.sb("b1", [P, E * STEPS])
        b2 = s.sb("b2", [P, C])
        index = s.sb("index", [P, TS], I32)
        xg = s.sb("xg", [P, TS, C])
        xT = s.sb("xT", [P, 2, 2, KC, CAP], F32R)
        w1_in = s.sb("w1_in", [P, 2, KC, 2 * P])
        w2_in = s.sb("w2_in", [P, 2, 2, C])
        w1 = s.sb("w1", [P, 2, 2, KC, P], F32R)
        w2 = s.sb("w2", [P, 2, 2, C], F32R)
        h = s.sb("h", [P, 2, CAP])
        hT = s.sb("hT", [P, 2, 2, CAP], F32R)
        out = s.sb("out", [P, TS, C])
        h_bank = [s.ps(f"h{i}") for i in range(2)]
        acc = [s.ps(f"acc{i}") for i in range(TS)]

        ident0, ident_ready = s.sem("ident0"), s.sem("ident_ready")
        in_x2 = s.sem("in_x2")
        in_b1, in_b2, b1_mm, b1_ready = s.sem("in_b1"), s.sem("in_b2"), s.sem("b1_mm"), s.sem("b1_ready")
        index_ready, gathered, waited = s.sem("index_ready"), s.sem("gathered"), s.sem("waited")
        x_mm, x_hi, x_ready = s.sem("x_mm"), s.sem("x_hi"), s.sem("x_ready")
        w_in = [s.sem(f"w_in{i}") for i in range(2)]
        w1_hi, w1_ready, w2_hi, w2_ready = s.sem("w1_hi"), s.sem("w1_ready"), s.sem("w2_hi"), s.sem("w2_ready")
        h_mm, h_ready, hT_hi, hT_ready = s.sem("h_mm"), s.sem("h_ready"), s.sem("hT_hi"), s.sem("hT_ready")
        o_mm, out_ready, stored = s.sem("o_mm"), s.sem("out_ready"), s.sem("stored")
        block = s.block()

        w1_v = a.w1.rearrange("e (k p) f -> e p k f", p=P)
        w2_v = a.w2.rearrange("e (i j p) c -> (e i) p j c", j=2, p=P)
        NT = z.TOK // P
        x2_v = a.x2.rearrange("(e t p) c -> e p t c", t=NT // E, p=P)

        @block.sync
        def _(sp):
            sp.dma_start(b1_rows[:, :], a.b1.rearrange("e (i p) -> (e i) p", p=P)).then_inc(in_b1, 16)
            with sp.Fori(0, E) as e:
                def load_quad(q):
                    eq = sp.snap(e * QUADS + q)
                    for buf in range(2):
                        sp.wait_ge(w1_ready, eq * 4 + buf * 2 - 2 + FREE)
                        sp.wait_ge(w2_ready, eq * 4 + buf * 2 - 2 + FREE)
                        sp.dma_start(w1_in[:, buf, :, :],
                                     w1_v[bass.ds(e, 1), :, :, bass.ds(q * (4 * P) + buf * 2 * P, 2 * P)]
                                     .rearrange("o p k f -> (o p) k f")).then_inc(w_in[buf], 16)
                        sp.dma_start(w2_in[:, buf, :, :], w2_v[bass.ds(eq * 2 + buf, 1), :, :, :]
                                     .rearrange("o p j c -> (o p) j c")).then_inc(w_in[buf], 16)

                load_quad(0)
                sp.dma_start(a.x2_sb[:, bass.ds(e * (NT // E), NT // E), :], x2_v[bass.ds(e, 1), :, :, :]
                             .rearrange("o p t c -> (o p) t c")).then_inc(in_x2, 16)
                sp.wait_ge(out_ready, e * TS)
                sp.dma_start(b2[:, :], a.b2[bass.ds(e, 1), :].broadcast_to([P, C])).then_inc(in_b2, 16)
                with sp.Fori(1, QUADS) as q:
                    load_quad(q)
            sp.wait_ge(in_x2, E * 16)

        @block.gpsimd
        def _(pool):
            make_ident(pool, ident, ident0, ident_ready)

            def gather(n, first, tiles, before):
                pool.tensor_copy(index[:, 0:tiles], a.tokens[:, bass.ds(first, tiles)]).then_inc(index_ready, 1)
                wait_alone(pool, index_ready, n + 1, waited)
                for t in range(tiles):
                    pool.indirect_dma_start(xg[:, t, :], None, a.x2,
                                            bass.IndirectOffsetOnAxis(ap=index[:, t:t + 1], axis=0)).then_inc(gathered, 16)
                pool.wait_ge(gathered, (before + tiles) * 16)

            gather(0, 0, TS, 0)
            with pool.Fori(0, E) as e:
                following = pool.snap((e + 1) % E * TS)
                with pool.Fori(0, TS // 2) as k:
                    before = pool.snap((e + 1) * TS + k * 2)
                    pool.wait_ge(x_mm, before)
                    gather(e * (TS // 2) + k + 1, pool.snap(following + k * 2), 2, before)
                pool.wait_ge(out_ready, (e + 1) * TS)
                pool.dma_start(a.eo[bass.ds(e * CAP, CAP), :].rearrange("(t p) c -> p t c", p=P),
                               out[:, :, :]).then_inc(stored, 16)
            pool.wait_ge(stored, E * 16)

        @block.scalar
        def _(act):
            act.wait_ge(b1_ready, 1)
            with act.Fori(0, E * QUADS) as eq:
                n = act.snap(eq * 4)
                n2 = act.snap(eq * 8)
                for j in range(4):
                    if j % 2 == 0:
                        act.wait_ge(w_in[j // 2], (eq + 1) * 32)
                    cols = slice(j % 2 * P, (j % 2 + 1) * P)
                    act.wait_ge(h_mm, n2 + 2 * j - 2 + 2 * FREE)
                    act.activation(w1[:, j % 2, 0, :, :], w1_in[:, j // 2, :, cols], ACT.Copy).then_inc(w1_hi, 1)
                    act.wait_ge(o_mm, n + j - 1 + FREE)
                    act.activation(w2[:, j % 2, 0, :], w2_in[:, j // 2, j % 2, :], ACT.Copy).then_inc(w2_hi, 1)
                    for half in range(2):
                        act.wait_ge(h_mm, n2 + 2 * j + half + 2 * FREE + 1)
                        act.wait_ge(hT_ready, n2 + 2 * j + half - 3 + 2 * FREE)
                        act.activation(h[:, j % 2, half * HALF:(half + 1) * HALF], h_bank[half][:, 0:HALF], ACT.Gelu,
                                       bias=b1[:, bass.ds(n + j, 1)]).then_inc(h_ready, 1)

        @block.vector
        def _(dve):
            dve.sem_inc(hT_ready, 2 * FREE)
            dve.sem_inc(w1_ready, FREE)
            dve.sem_inc(w2_ready, FREE)
            dve.wait_ge(b1_mm, 1)
            dve.tensor_copy(b1[:, :], acc[0][:, 0:E * STEPS]).then_inc(b1_ready, 1)

            def split_x(e, t, buf, bank):
                cols = bass.ds(t * P, P)
                src = bank[:, :].rearrange("p (k q) -> p k q", k=KC)
                dve.wait_ge(x_mm, e * TS + t + 1)
                dve.tensor_scalar(xT[:, buf, 0, :, cols], src, 0.0, None, ALU.add).then_inc(x_hi, 1)
                dve.wait_ge(x_hi, e * TS + t + 1)
                dve.tensor_tensor(xT[:, buf, 1, :, cols], src, xT[:, buf, 0, :, cols].bitcast(F32), ALU.subtract).then_inc(x_ready, 1)

            def quad(e, par, q, tile):
                eq = dve.snap(e * QUADS + q)
                n = dve.snap(eq * 4)
                n2 = dve.snap(eq * 8)
                for j in range(4):
                    cols = slice(j % 2 * P, (j % 2 + 1) * P)
                    dve.wait_ge(w1_hi, n + j + 1)
                    dve.tensor_tensor(w1[:, j % 2, 1, :, :], w1_in[:, j // 2, :, cols], w1[:, j % 2, 0, :, :].bitcast(F32), ALU.subtract).then_inc(w1_ready, 1)
                    dve.wait_ge(w2_hi, n + j + 1)
                    dve.tensor_tensor(w2[:, j % 2, 1, :], w2_in[:, j // 2, j % 2, :], w2[:, j % 2, 0, :].bitcast(F32), ALU.subtract).then_inc(w2_ready, 1)
                    dve.wait_ge(o_mm, n + j - 1 + FREE)
                    for half in range(2):
                        cols = slice(half * HALF, (half + 1) * HALF)
                        dve.wait_ge(h_ready, n2 + 2 * j + half + 1)
                        dve.tensor_copy(hT[:, j % 2, 0, cols], h[:, j % 2, cols]).then_inc(hT_hi, 1)
                        dve.wait_ge(hT_hi, n2 + 2 * j + half + 1)
                        dve.tensor_tensor(hT[:, j % 2, 1, cols], h[:, j % 2, cols], hT[:, j % 2, 0, cols].bitcast(F32), ALU.subtract).then_inc(hT_ready, 1)
                    if tile is not None and j < 2:
                        split_x(dve.snap(e + 1), tile + j, 1 - par, h_bank[0])

            for t in range(TS):
                split_x(0, t, 0, h_bank[t % 2])
            with dve.Fori(0, E // 2) as pair:
                for par in range(2):
                    e = dve.snap(pair * 2 + par)
                    quad(e, par, 0, None)
                    with dve.Fori(1, QUADS) as q:
                        quad(e, par, q, dve.snap(q * 2 - 2))
                    dve.wait_ge(in_b2, (e + 1) * 16)
                    dve.wait_ge(stored, e * 16)
                    dve.wait_ge(o_mm, (e + 1) * STEPS + FREE)
                    for t in range(TS):
                        dve.tensor_tensor(out[:, t, :], acc[t][:, :], b2[:, :], ALU.add).then_inc(out_ready, 1)

        @block.tensor
        def _(pe):
            pe.sem_inc(h_mm, 2 * FREE)
            pe.sem_inc(o_mm, FREE)
            pe.wait_ge(ident_ready, 1)
            pe.wait_ge(in_b1, 16)
            pe.transpose(acc[0][:, 0:E * STEPS], b1_rows[:, :], ident[0:E * STEPS, 0:E * STEPS]).then_inc(b1_mm, 1)

            def transpose_rows(bank, rows):
                for k in range(KC):
                    last = pe.transpose(bank[:, k * P:(k + 1) * P], rows[:, k * P:(k + 1) * P], ident[:, :])
                last.then_inc(x_mm, 1)

            def first_layer(n, n2, j, buf, opens=False, tiles=None):
                pe.wait_ge(w1_ready, n + j + 1 + FREE)
                if tiles is not None:
                    pe.wait_ge(x_ready, tiles)
                for half in range(2):
                    if not opens:
                        pe.wait_ge(h_ready, n2 + 2 * j + half - 1)
                    for i, (pw, px) in enumerate(PARTS):
                        for k in range(KC):
                            last = pe.matmul(h_bank[half][:, 0:HALF], w1[:, j % 2, pw, k, :],
                                             xT[:, buf, px, k, half * HALF:(half + 1) * HALF],
                                             start=(i == 0 and k == 0), stop=(i == 2 and k == KC - 1))
                    last.then_inc(h_mm, 1)

            def second_layer(n, n2, j, start=False, stop=False, between=None):
                pe.wait_ge(w2_ready, n + j + 1 + FREE)
                pe.wait_ge(hT_ready, n2 + 2 * j + 2 + 2 * FREE)
                for t in range(TS):
                    for i, (ph, pw) in enumerate(PARTS):
                        last = pe.matmul(acc[t][:, :], hT[:, j % 2, ph, t * P:(t + 1) * P], w2[:, j % 2, pw, :],
                                         start=(start and i == 0), stop=(stop and i == 2))
                    if between is not None and t == 1:
                        between()
                last.then_inc(o_mm, 1)

            for t in range(TS):
                if t == 0:
                    pe.wait_ge(gathered, TS * 16)
                if t >= 2:
                    pe.wait_ge(x_ready, t - 1)
                transpose_rows(h_bank[t % 2], xg[:, t, :])
            pe.wait_ge(x_ready, TS)
            with pe.Fori(0, E // 2) as pair:
                for par in range(2):
                    e = pe.snap(pair * 2 + par)
                    n, n2 = pe.snap(e * STEPS), pe.snap(e * (2 * STEPS))
                    for j in range(4):
                        if j == 0:
                            pe.wait_ge(h_ready, n2)
                        first_layer(n, n2, j, par, opens=(j == 0))
                        if j == 1:
                            pe.wait_ge(out_ready, e * TS)
                        if j >= 1:
                            second_layer(n, n2, j - 1, start=(j == 1))
                    with pe.Fori(1, QUADS) as q:
                        m, m2 = pe.snap((e * QUADS + q) * 4), pe.snap((e * QUADS + q) * 8)
                        tile = pe.snap(q * 2 - 2)
                        for j in range(4):
                            before = (e + 1) * TS + tile + j

                            def next_rows():
                                pe.wait_ge(h_ready, m2 + 2 * j + 1)
                                if j == 0:
                                    pe.wait_ge(gathered, ((e + 1) * TS + tile + 2) * 16)
                                transpose_rows(h_bank[0], xg[:, j, :])

                            first_layer(m, m2, j, par, tiles=before if 1 <= j <= 2 else None)
                            second_layer(m, m2, j - 1, between=next_rows if j < 2 else None)
                    second_layer(n, n2, STEPS - 1, stop=True)


def combine(nc, z, a):
    C, NT = z.C, z.TOK // P
    TG = 4
    GROUPS = NT // TG
    EPS = 1e-5

    with ExitStack() as ctx:
        s = Stage(nc, ctx, "cb")
        index = s.sb("index", [P, 2, TG], I32)
        y = s.sb("y", [P, 2, TG, C])
        r = s.sb("r", [P, 2, TG, C])
        o = s.sb("o", [P, 2, TG, C])
        stat = s.sb("stat", [P, 2, TG, 6])
        mv = s.sb("mv", [P, 2, TG, 2])
        var_eps, rstd = s.sb("var_eps", [P, 2, TG]), s.sb("rstd", [P, 2, TG])
        minus_half = s.sb("minus_half", [P, TG])

        in_y = [s.sem(f"in_y{i}") for i in range(2)]
        out_o = [s.sem(f"out_o{i}") for i in range(2)]
        half_ready, index_ready, r_ready, stat_ready = s.sem("half_ready"), s.sem("index_ready"), s.sem("r_ready"), s.sem("stat_ready")
        mv_ready, var_ready, rstd_ready, o_ready = s.sem("mv_ready"), s.sem("var_ready"), s.sem("rstd_ready"), s.sem("o_ready")
        waited = [s.sem("waited_dve"), s.sem("waited_pool")]
        block = s.block()
        out_v = a.out.rearrange("b n c -> (b n) c").rearrange("(g t p) c -> g p t c", t=TG, p=P)

        @block.gpsimd
        def _(pool):
            pool.memset(minus_half[:, :], -0.5).then_inc(half_ready, 1)
            pool.wait_ge(half_ready, 1)

            def gather(n, par):
                pool.tensor_copy(index[:, par, :], a.slots[:, bass.ds(n * TG, TG)]).then_inc(index_ready, 1)
                wait_alone(pool, index_ready, n + 1, waited[1])
                for t in range(TG):
                    pool.indirect_dma_start(y[:, par, t, :], None, a.eo,
                                            bass.IndirectOffsetOnAxis(ap=index[:, par, t:t + 1], axis=0)).then_inc(in_y[par], 16)

            def rstds(n, par):
                pool.wait_ge(var_ready, n + 1)
                pool.tensor_tensor(rstd[:, par, :], var_eps[:, par, :], minus_half[:, :], ALU.pow).then_inc(rstd_ready, 1)

            for par in range(2):
                gather(par, par)
            with pool.Fori(0, GROUPS // 2 - 1) as i:
                for par in range(2):
                    n = pool.snap(i * 2 + par)
                    rstds(n, par)
                    gather(pool.snap(n + 2), par)
            for par in range(2):
                rstds(GROUPS - 2 + par, par)

        @block.vector
        def _(dve):
            with dve.Fori(0, GROUPS // 2) as i:
                for par in range(2):
                    n = dve.snap(i * 2 + par)
                    dve.wait_ge(in_y[par], (i + 1) * (16 * TG))
                    for t in range(TG):
                        if t == 0:
                            dve.wait_ge(o_ready, n * TG)
                        dve.scalar_tensor_tensor(out=r[:, par, t, :], in0=y[:, par, t, :],
                                                 scalar=a.weights[:, bass.ds(n * TG + t, 1)],
                                                 in1=a.x2_sb[:, bass.ds(n * TG + t, 1), :].rearrange("p o c -> p (o c)"),
                                                 op0=ALU.mult, op1=ALU.add).then_inc(r_ready, 1)
                        dve.wait_ge(r_ready, n * TG + t + 1)
                        dve.bn_stats(stat[:, par, t, :], r[:, par, t, :]).then_inc(stat_ready, 1)
                    wait_alone(dve, stat_ready, (n + 1) * TG, waited[0])
                    for t in range(TG):
                        dve.bn_aggr(mv[:, par, t, :], stat[:, par, t, :]).then_inc(mv_ready, 1)
                    dve.wait_ge(mv_ready, (n + 1) * TG)
                    dve.tensor_scalar(var_eps[:, par, :], mv[:, par, :, 1], EPS, None, ALU.add).then_inc(var_ready, 1)
                    dve.wait_ge(rstd_ready, n + 1)
                    dve.wait_ge(out_o[par], i * 16)
                    for t in range(TG):
                        dve.tensor_scalar(o[:, par, t, :], r[:, par, t, :], mv[:, par, t, 0:1], rstd[:, par, t:t + 1],
                                          ALU.subtract, ALU.mult).then_inc(o_ready, 1)

        @block.scalar
        def _(act):
            with act.Fori(0, GROUPS // 2) as i:
                for par in range(2):
                    act.wait_ge(o_ready, (i * 2 + par + 1) * TG)
                    act.dma_start(out_v[bass.ds(i * 2 + par, 1), :, :, :].rearrange("o p t c -> (o p) t c"),
                                  o[:, par, :, :]).then_inc(out_o[par], 16)
            for par in range(2):
                act.wait_ge(out_o[par], GROUPS // 2 * 16)


class Tensors:
    pass


def decoder_layer(nc, x, ctx_rows, qkv_w, qkv_b, proj_w, proj_b, Wq, Wk, Wv, Wo, bo, gx, bx, gl, bl,
                  router_w, w1, b1, w2, b2, out):
    z = Shapes(x, ctx_rows, w1)
    slots = z.E * z.CAP

    def scratch(name, shape, dt=F32):
        return nc.dram_tensor(name, shape, dt, kind="Internal").ap()

    xT = scratch("xT", (z.B, z.C, z.N))
    attnT = scratch("attnT", (z.B, z.C, z.N))
    transpose_x(nc, z, x, xT)
    self_attention(nc, z, xT, qkv_w, qkv_b, attnT)
    with ExitStack() as ctx:
        keep = Stage(nc, ctx, "keep")
        NT = z.TOK // P
        a = Tensors()
        a.x, a.ctx, a.attnT, a.out = x, ctx_rows, attnT, out
        a.proj_w, a.proj_b, a.Wq, a.Wk, a.Wv, a.Wo, a.bo = proj_w, proj_b, Wq, Wk, Wv, Wo, bo
        a.gx, a.bx, a.gl, a.bl, a.rw = gx, bx, gl, bl, router_w
        a.w1, a.b1, a.w2, a.b2 = w1, b1, w2, b2
        a.x2 = scratch("x2", (z.TOK, z.C))
        a.table = scratch("table", (slots, 1), I32)
        a.eo = scratch("eo", (slots, z.C))
        a.logits = keep.sb("logits", [P, NT, z.E])
        a.weights = keep.sb("weights", [P, NT])
        a.slots = keep.sb("slots", [P, NT], I32)
        a.tokens = keep.sb("tokens", [P, slots // P], I32)
        cross_attention(nc, z, a)
        route(nc, z, a)
        a.x2_sb = keep.sb("x2_sb", [P, NT, z.C])
        experts(nc, z, a)
        combine(nc, z, a)


_INS = ["x", "ctx_1024", "L0_attn_qkv_w", "L0_attn_qkv_b", "L0_attn_proj_w", "L0_attn_proj_b",
        "L0_xattn_Wq", "L0_xattn_Wk", "L0_xattn_Wv", "L0_xattn_Wo", "L0_xattn_bo", "L0_xattn_gx",
        "L0_xattn_bx", "L0_xattn_gl", "L0_xattn_bl", "L0_ffn_router_w", "L0_ffn_w1", "L0_ffn_b1",
        "L0_ffn_w2", "L0_ffn_b2"]
_OUTS = [((2, 2048, 512), "float32")]


def kernel(**inputs):
    import numpy as _np
    import concourse.bacc as _bacc
    from concourse import mybir as _mybir
    from concourse.bass_utils import run_bass_kernel_spmd as _run

    nc = _bacc.Bacc("TRN2", target_bir_lowering=False, num_devices=1)
    nc.disable_value_cache = True
    arrays, args = {}, []
    for name in _INS:
        a = _np.ascontiguousarray(inputs[name])
        arrays[f"in_{name}_dram"] = a
        args.append(nc.dram_tensor(f"in_{name}_dram", a.shape, _mybir.dt.from_np(a.dtype), kind="ExternalInput").ap())
    for i, (shape, dtype) in enumerate(_OUTS):
        dt = _mybir.dt.from_np(_np.dtype(dtype))
        args.append(nc.dram_tensor(f"out_{i}_dram", shape, dt, kind="ExternalOutput").ap())
    decoder_layer(nc, *args)
    r = _run(nc, [arrays], core_ids=[0])
    return r.results[0]["out_0_dram"]
```
